# Optimizing a Trainium2 kernel written in Bass

```python
import numpy as np
import jax
import jax.numpy as jnp

def _softmax(x, axis=-1):
    return jax.nn.softmax(x, axis=axis)

def _gelu(x):
    return jax.nn.gelu(x, approximate=True)

def _silu(x):
    return jax.nn.silu(x)

def _sigmoid(x):
    return jax.nn.sigmoid(x)

def _layernorm(x, axis=-1, eps=1e-05):
    m = jnp.mean(x, axis=axis, keepdims=True)
    v = jnp.var(x, axis=axis, keepdims=True)
    return (x - m) / jnp.sqrt(v + eps)

def _scatter_add(tgt, idx, src, axis=0):
    return tgt.at[idx].add(src)

def _segment_sum(src, seg, n):
    return jax.ops.segment_sum(src, seg, n)
kernel_name = 'mk_xattn_seq_d4_seqx_r8_913f70'

def setup_inputs(seed: int=0):
    np.random.seed(seed)
    _w = jnp.asarray

    def _rec_inputs():
        import jax
        import jax.numpy as jnp
        _rk = jax.random.key(seed)
        x = -0.000125 + 0.9999 * jax.random.normal(jax.random.fold_in(_rk, 1), (4, 512, 128), jnp.float32)
        _lenS = 512 - jax.random.randint(jax.random.fold_in(_rk, 7), (4,), 0, max(1, 512 // 4) + 1, jnp.int32)
        _lenS2 = 77 - jax.random.randint(jax.random.fold_in(_rk, 8), (4,), 0, max(1, 77 // 4) + 1, jnp.int32)
        _ctx_2048P = jax.random.normal(jax.random.fold_in(_rk, 11), (4, 16, 256), jnp.float32)
        _ctx_2048c = jax.random.dirichlet(jax.random.fold_in(_rk, 511), 0.3 * jnp.ones((16,), jnp.float32), (4, 77))
        _ctx_2048t = jnp.einsum('bsk,bkd->bsd', _ctx_2048c, _ctx_2048P)
        _ctx_2048t = _ctx_2048t * jax.lax.rsqrt(jnp.mean(jnp.square(_ctx_2048t)) + 1e-12) * 0.953939
        ctx_2048 = 5.36139e-06 + 1.00015 * (_ctx_2048t + 0.3 * jax.random.normal(jax.random.fold_in(_rk, 611), (4, 77, 256), jnp.float32))
        _validS = jnp.arange(512)[None, :] < _lenS[:, None]
        _validS2 = jnp.arange(77)[None, :] < _lenS2[:, None]
        _causal = jnp.tril(jnp.ones((512, 512), dtype=bool))
        mask_S_fk1 = jnp.where(_validS[0], 1.0, 0.0).astype(jnp.float32)
        mask_S_fk0 = jnp.where(_validS[0], 0.0, 1.0).astype(jnp.float32)
        return (x, ctx_2048, mask_S_fk1, mask_S_fk0)
    x, ctx_2048, mask_S_fk1, mask_S_fk0 = _rec_inputs()

    def _L0_xattn_setup():
        import jax, jax.numpy as jnp
        import numpy as np
        HEADS = 16
        HEAD_DIM = 64
        SUPPRESS = 20.0
        key = jax.random.key(seed)
        ks = jax.random.split(key, 8)
        B, HW, C, T, CT = (8, 512, 128, 77, 256)
        inner = HEADS * HEAD_DIM
        scale = 0.02
        return {'hidden_states': jax.random.normal(ks[0], (B, HW, C), jnp.float32), 'encoder_hidden_states': jax.random.normal(ks[1], (B, T, CT), jnp.float32), 'mask_A': (jax.random.uniform(ks[2], (HW,)) > 0.5).astype(jnp.float32), 'mask_B': (jax.random.uniform(ks[3], (HW,)) > 0.5).astype(jnp.float32), 'Wq': jax.random.normal(ks[4], (C, inner), jnp.float32) * scale, 'Wk': jax.random.normal(ks[5], (CT, inner), jnp.float32) * scale, 'Wv': jax.random.normal(ks[6], (CT, inner), jnp.float32) * scale, 'Wo': jax.random.normal(ks[7], (inner, C), jnp.float32) * scale, 'bo': jnp.zeros((C,), jnp.float32), 'token_indices_A': jnp.array([2, 3], dtype=jnp.int64), 'token_indices_B': jnp.array([5, 6], dtype=jnp.int64)}
    _L0_xattn_all = _L0_xattn_setup()
    _L0_xattn_in = {k: v for k, v in _L0_xattn_all.items() if k in ('Wq', 'Wk', 'Wv', 'Wo', 'bo', 'token_indices_A', 'token_indices_B')}
    del _L0_xattn_all

    def _L1_xattn_setup():
        import jax, jax.numpy as jnp
        import numpy as np
        D_MODEL = 128
        N_HEADS = 16
        N_KV_HEADS = 4
        HEAD_DIM = D_MODEL // N_HEADS
        SPEAKER_DIM = 256
        EPS = 1e-05

        def rmsnorm(x, w, eps=EPS):
            xf = x.astype(jnp.float32)
            inv = jax.lax.rsqrt(jnp.mean(xf * xf, axis=-1, keepdims=True) + eps)
            return (xf * inv).astype(x.dtype) * w
        key = jax.random.key(seed)
        ks = jax.random.split(key, 7)
        B, T, S = (4, 256, 64)
        x = jax.random.normal(ks[0], (B, T, D_MODEL), dtype=jnp.float32)
        cond = jax.random.normal(ks[1], (B, S, SPEAKER_DIM), dtype=jnp.float32)
        sq = 0.02
        wq = jax.random.normal(ks[2], (D_MODEL, N_HEADS * HEAD_DIM), dtype=jnp.float32) * sq
        wk = jax.random.normal(ks[3], (SPEAKER_DIM, N_KV_HEADS * HEAD_DIM), dtype=jnp.float32) * sq
        wv = jax.random.normal(ks[4], (SPEAKER_DIM, N_KV_HEADS * HEAD_DIM), dtype=jnp.float32) * sq
        wo = jax.random.normal(ks[5], (N_HEADS * HEAD_DIM, D_MODEL), dtype=jnp.float32) * sq
        norm_w = jnp.ones((D_MODEL,), dtype=jnp.float32)
        return {'x': x, 'cond': cond, 'wq': wq, 'wk': wk, 'wv': wv, 'wo': wo, 'norm_w': norm_w}
    _L1_xattn_all = _L1_xattn_setup()
    _L1_xattn_in = {k: v for k, v in _L1_xattn_all.items() if k in ('wq', 'wk', 'wv', 'wo', 'norm_w')}
    del _L1_xattn_all

    def _L2_xattn_setup():
        import jax, jax.numpy as jnp
        import numpy as np
        HEADS = 16
        HEAD_DIM = 64
        SUPPRESS = 20.0
        key = jax.random.key(seed)
        ks = jax.random.split(key, 8)
        B, HW, C, T, CT = (8, 512, 128, 77, 256)
        inner = HEADS * HEAD_DIM
        scale = 0.02
        return {'hidden_states': jax.random.normal(ks[0], (B, HW, C), jnp.float32), 'encoder_hidden_states': jax.random.normal(ks[1], (B, T, CT), jnp.float32), 'mask_A': (jax.random.uniform(ks[2], (HW,)) > 0.5).astype(jnp.float32), 'mask_B': (jax.random.uniform(ks[3], (HW,)) > 0.5).astype(jnp.float32), 'Wq': jax.random.normal(ks[4], (C, inner), jnp.float32) * scale, 'Wk': jax.random.normal(ks[5], (CT, inner), jnp.float32) * scale, 'Wv': jax.random.normal(ks[6], (CT, inner), jnp.float32) * scale, 'Wo': jax.random.normal(ks[7], (inner, C), jnp.float32) * scale, 'bo': jnp.zeros((C,), jnp.float32), 'token_indices_A': jnp.array([2, 3], dtype=jnp.int64), 'token_indices_B': jnp.array([5, 6], dtype=jnp.int64)}
    _L2_xattn_all = _L2_xattn_setup()
    _L2_xattn_in = {k: v for k, v in _L2_xattn_all.items() if k in ('Wq', 'Wk', 'Wv', 'Wo', 'bo', 'token_indices_A', 'token_indices_B')}
    del _L2_xattn_all

    def _L3_xattn_setup():
        import jax, jax.numpy as jnp
        import numpy as np
        HEADS = 16
        HEAD_DIM = 64
        SUPPRESS = 20.0
        key = jax.random.key(seed)
        ks = jax.random.split(key, 8)
        B, HW, C, T, CT = (8, 512, 128, 77, 256)
        inner = HEADS * HEAD_DIM
        scale = 0.02
        return {'hidden_states': jax.random.normal(ks[0], (B, HW, C), jnp.float32), 'encoder_hidden_states': jax.random.normal(ks[1], (B, T, CT), jnp.float32), 'mask_A': (jax.random.uniform(ks[2], (HW,)) > 0.5).astype(jnp.float32), 'mask_B': (jax.random.uniform(ks[3], (HW,)) > 0.5).astype(jnp.float32), 'Wq': jax.random.normal(ks[4], (C, inner), jnp.float32) * scale, 'Wk': jax.random.normal(ks[5], (CT, inner), jnp.float32) * scale, 'Wv': jax.random.normal(ks[6], (CT, inner), jnp.float32) * scale, 'Wo': jax.random.normal(ks[7], (inner, C), jnp.float32) * scale, 'bo': jnp.zeros((C,), jnp.float32), 'token_indices_A': jnp.array([2, 3], dtype=jnp.int64), 'token_indices_B': jnp.array([5, 6], dtype=jnp.int64)}
    _L3_xattn_all = _L3_xattn_setup()
    _L3_xattn_in = {k: v for k, v in _L3_xattn_all.items() if k in ('Wq', 'Wk', 'Wv', 'Wo', 'bo', 'token_indices_A', 'token_indices_B')}
    del _L3_xattn_all
    return {'x': x, 'ctx_2048': ctx_2048, 'mask_S_fk1': mask_S_fk1, 'mask_S_fk0': mask_S_fk0, 'L0_xattn_Wq': _L0_xattn_in['Wq'], 'L0_xattn_Wk': _L0_xattn_in['Wk'], 'L0_xattn_Wv': _L0_xattn_in['Wv'], 'L0_xattn_Wo': _L0_xattn_in['Wo'], 'L0_xattn_bo': _L0_xattn_in['bo'], 'L0_xattn_token_indices_A': _L0_xattn_in['token_indices_A'], 'L0_xattn_token_indices_B': _L0_xattn_in['token_indices_B'], 'L1_xattn_wq': _L1_xattn_in['wq'], 'L1_xattn_wk': _L1_xattn_in['wk'], 'L1_xattn_wv': _L1_xattn_in['wv'], 'L1_xattn_wo': _L1_xattn_in['wo'], 'L1_xattn_norm_w': _L1_xattn_in['norm_w'], 'L2_xattn_Wq': _L2_xattn_in['Wq'], 'L2_xattn_Wk': _L2_xattn_in['Wk'], 'L2_xattn_Wv': _L2_xattn_in['Wv'], 'L2_xattn_Wo': _L2_xattn_in['Wo'], 'L2_xattn_bo': _L2_xattn_in['bo'], 'L2_xattn_token_indices_A': _L2_xattn_in['token_indices_A'], 'L2_xattn_token_indices_B': _L2_xattn_in['token_indices_B'], 'L3_xattn_Wq': _L3_xattn_in['Wq'], 'L3_xattn_Wk': _L3_xattn_in['Wk'], 'L3_xattn_Wv': _L3_xattn_in['Wv'], 'L3_xattn_Wo': _L3_xattn_in['Wo'], 'L3_xattn_bo': _L3_xattn_in['bo'], 'L3_xattn_token_indices_A': _L3_xattn_in['token_indices_A'], 'L3_xattn_token_indices_B': _L3_xattn_in['token_indices_B']}

def reference(x, ctx_2048, mask_S_fk1, mask_S_fk0, L0_xattn_Wq, L0_xattn_Wk, L0_xattn_Wv, L0_xattn_Wo, L0_xattn_bo, L0_xattn_token_indices_A, L0_xattn_token_indices_B, L1_xattn_wq, L1_xattn_wk, L1_xattn_wv, L1_xattn_wo, L1_xattn_norm_w, L2_xattn_Wq, L2_xattn_Wk, L2_xattn_Wv, L2_xattn_Wo, L2_xattn_bo, L2_xattn_token_indices_A, L2_xattn_token_indices_B, L3_xattn_Wq, L3_xattn_Wk, L3_xattn_Wv, L3_xattn_Wo, L3_xattn_bo, L3_xattn_token_indices_A, L3_xattn_token_indices_B):
    import jax
    import jax.numpy as jnp

    def _L0_xattn_ref(hidden_states, encoder_hidden_states, mask_A, mask_B, Wq, Wk, Wv, Wo, bo, token_indices_A, token_indices_B):
        import jax, jax.numpy as jnp
        import numpy as np
        HEADS = 16
        HEAD_DIM = 64
        SUPPRESS = 20.0
        B, HW, C = hidden_states.shape
        T = encoder_hidden_states.shape[1]
        residual = hidden_states
        q = hidden_states @ Wq
        k = encoder_hidden_states @ Wk
        v = encoder_hidden_states @ Wv
        q = q.reshape(B, HW, HEADS, HEAD_DIM).transpose(0, 2, 1, 3)
        k = k.reshape(B, T, HEADS, HEAD_DIM).transpose(0, 2, 1, 3)
        v = v.reshape(B, T, HEADS, HEAD_DIM).transpose(0, 2, 1, 3)
        scale = HEAD_DIM ** (-0.5)
        logits = jnp.einsum('bhqd,bhkd->bhqk', q, k) * scale
        suppress_A_in = 1.0 - mask_A
        suppress_B_in = 1.0 - mask_B
        col_bias = jnp.zeros((HW, T), logits.dtype)
        col_bias = col_bias.at[:, token_indices_A].set((-SUPPRESS * suppress_A_in)[:, None])
        col_bias = col_bias.at[:, token_indices_B].set((-SUPPRESS * suppress_B_in)[:, None])
        logits = logits + col_bias[None, None, :, :]
        probs = jax.nn.softmax(logits, axis=-1)
        out = jnp.einsum('bhqk,bhkd->bhqd', probs, v)
        out = out.transpose(0, 2, 1, 3).reshape(B, HW, HEADS * HEAD_DIM)
        out = out @ Wo + bo
        out = out + residual
        return out

    def _L1_xattn_ref(x, cond, wq, wk, wv, wo, norm_w):
        import jax, jax.numpy as jnp
        import numpy as np
        D_MODEL = 128
        N_HEADS = 16
        N_KV_HEADS = 4
        HEAD_DIM = D_MODEL // N_HEADS
        SPEAKER_DIM = 256
        EPS = 1e-05

        def rmsnorm(x, w, eps=EPS):
            xf = x.astype(jnp.float32)
            inv = jax.lax.rsqrt(jnp.mean(xf * xf, axis=-1, keepdims=True) + eps)
            return (xf * inv).astype(x.dtype) * w
        B, T, _ = x.shape
        S = cond.shape[1]
        n_rep = N_HEADS // N_KV_HEADS
        residual = x
        xn = rmsnorm(x, norm_w)
        q = (xn @ wq).reshape(B, T, N_HEADS, HEAD_DIM)
        k = (cond @ wk).reshape(B, S, N_KV_HEADS, HEAD_DIM)
        v = (cond @ wv).reshape(B, S, N_KV_HEADS, HEAD_DIM)
        qg = q.reshape(B, T, N_KV_HEADS, n_rep, HEAD_DIM)
        scale = 1.0 / np.sqrt(HEAD_DIM).astype(np.float32)
        scores = jnp.einsum('btgrd,bsgd->bgrts', qg, k) * scale
        attn = jax.nn.softmax(scores.astype(jnp.float32), axis=-1).astype(q.dtype)
        out = jnp.einsum('bgrts,bsgd->btgrd', attn, v).reshape(B, T, N_HEADS * HEAD_DIM)
        return residual + out @ wo

    def _L2_xattn_ref(hidden_states, encoder_hidden_states, mask_A, mask_B, Wq, Wk, Wv, Wo, bo, token_indices_A, token_indices_B):
        import jax, jax.numpy as jnp
        import numpy as np
        HEADS = 16
        HEAD_DIM = 64
        SUPPRESS = 20.0
        B, HW, C = hidden_states.shape
        T = encoder_hidden_states.shape[1]
        residual = hidden_states
        q = hidden_states @ Wq
        k = encoder_hidden_states @ Wk
        v = encoder_hidden_states @ Wv
        q = q.reshape(B, HW, HEADS, HEAD_DIM).transpose(0, 2, 1, 3)
        k = k.reshape(B, T, HEADS, HEAD_DIM).transpose(0, 2, 1, 3)
        v = v.reshape(B, T, HEADS, HEAD_DIM).transpose(0, 2, 1, 3)
        scale = HEAD_DIM ** (-0.5)
        logits = jnp.einsum('bhqd,bhkd->bhqk', q, k) * scale
        suppress_A_in = 1.0 - mask_A
        suppress_B_in = 1.0 - mask_B
        col_bias = jnp.zeros((HW, T), logits.dtype)
        col_bias = col_bias.at[:, token_indices_A].set((-SUPPRESS * suppress_A_in)[:, None])
        col_bias = col_bias.at[:, token_indices_B].set((-SUPPRESS * suppress_B_in)[:, None])
        logits = logits + col_bias[None, None, :, :]
        probs = jax.nn.softmax(logits, axis=-1)
        out = jnp.einsum('bhqk,bhkd->bhqd', probs, v)
        out = out.transpose(0, 2, 1, 3).reshape(B, HW, HEADS * HEAD_DIM)
        out = out @ Wo + bo
        out = out + residual
        return out

    def _L3_xattn_ref(hidden_states, encoder_hidden_states, mask_A, mask_B, Wq, Wk, Wv, Wo, bo, token_indices_A, token_indices_B):
        import jax, jax.numpy as jnp
        import numpy as np
        HEADS = 16
        HEAD_DIM = 64
        SUPPRESS = 20.0
        B, HW, C = hidden_states.shape
        T = encoder_hidden_states.shape[1]
        residual = hidden_states
        q = hidden_states @ Wq
        k = encoder_hidden_states @ Wk
        v = encoder_hidden_states @ Wv
        q = q.reshape(B, HW, HEADS, HEAD_DIM).transpose(0, 2, 1, 3)
        k = k.reshape(B, T, HEADS, HEAD_DIM).transpose(0, 2, 1, 3)
        v = v.reshape(B, T, HEADS, HEAD_DIM).transpose(0, 2, 1, 3)
        scale = HEAD_DIM ** (-0.5)
        logits = jnp.einsum('bhqd,bhkd->bhqk', q, k) * scale
        suppress_A_in = 1.0 - mask_A
        suppress_B_in = 1.0 - mask_B
        col_bias = jnp.zeros((HW, T), logits.dtype)
        col_bias = col_bias.at[:, token_indices_A].set((-SUPPRESS * suppress_A_in)[:, None])
        col_bias = col_bias.at[:, token_indices_B].set((-SUPPRESS * suppress_B_in)[:, None])
        logits = logits + col_bias[None, None, :, :]
        probs = jax.nn.softmax(logits, axis=-1)
        out = jnp.einsum('bhqk,bhkd->bhqd', probs, v)
        out = out.transpose(0, 2, 1, 3).reshape(B, HW, HEADS * HEAD_DIM)
        out = out @ Wo + bo
        out = out + residual
        return out
    x = _L0_xattn_ref(x, ctx_2048, mask_S_fk1, mask_S_fk0, L0_xattn_Wq, L0_xattn_Wk, L0_xattn_Wv, L0_xattn_Wo, L0_xattn_bo, L0_xattn_token_indices_A, L0_xattn_token_indices_B)
    x = _L1_xattn_ref(x, ctx_2048, L1_xattn_wq, L1_xattn_wk, L1_xattn_wv, L1_xattn_wo, L1_xattn_norm_w)
    x = _L2_xattn_ref(x, ctx_2048, mask_S_fk1, mask_S_fk0, L2_xattn_Wq, L2_xattn_Wk, L2_xattn_Wv, L2_xattn_Wo, L2_xattn_bo, L2_xattn_token_indices_A, L2_xattn_token_indices_B)
    x = _L3_xattn_ref(x, ctx_2048, mask_S_fk1, mask_S_fk0, L3_xattn_Wq, L3_xattn_Wk, L3_xattn_Wv, L3_xattn_Wo, L3_xattn_bo, L3_xattn_token_indices_A, L3_xattn_token_indices_B)
    return x

_drawn_inputs = setup_inputs


def setup_inputs(seed=0):
    import zlib

    import numpy as np

    out = dict(_drawn_inputs(seed))
    spreads = {'L0_xattn_bo': (0.0, 0.1),
     'L1_xattn_norm_w': (1.0, 0.6),
     'L2_xattn_bo': (0.0, 0.1),
     'L3_xattn_bo': (0.0, 0.1)}
    factors = {'mask_S_fk1': 8.0,
     'mask_S_fk0': 8.0,
     'L0_xattn_Wq': 8.0,
     'L0_xattn_Wk': 8.0,
     'L1_xattn_wq': 8.0,
     'L1_xattn_wk': 8.0,
     'L2_xattn_Wq': 8.0,
     'L2_xattn_Wk': 8.0,
     'L3_xattn_Wq': 8.0,
     'L3_xattn_Wk': 8.0}
    for name, (base, spread) in spreads.items():
        noise = np.random.default_rng([zlib.crc32(name.encode()), seed]).standard_normal(out[name].shape)
        drawn = base * np.exp(spread * noise) if base else spread * noise
        out[name] = jnp.asarray(drawn.astype(out[name].dtype))
    for name, factor in factors.items():
        out[name] = (out[name] * factor).astype(out[name].dtype)
    return out
```

```python
from contextlib import ExitStack

import concourse.bass as bass
from concourse import mybir

F32 = mybir.dt.float32
F32R = mybir.dt.float32r
BF16 = mybir.dt.bfloat16
I32 = mybir.dt.int32
ALU = mybir.AluOpType
ACT = mybir.ActivationFunctionType
AX = mybir.AxisListType

LAYERS = 4
BATCH, SEQ, C = 4, 512, 128
KEYS, CTX = 77, 256
HEADS, HDIM = 16, 64
INNER = HEADS * HDIM
P = 128
TILES = BATCH * SEQ // P
TPB = SEQ // P
HK = HEADS * KEYS
BK = BATCH * KEYS
CHUNKS = [(c * P, min(P, HK - c * P)) for c in range((HK + P - 1) // P)]
QUADS = [CHUNKS[0:4], CHUNKS[4:8], CHUNKS[8:10]]
GROUPS = [(0, 6), (6, 6), (12, 4)]
NG, NQ = len(GROUPS), len(QUADS)
KC = CTX // P
PAIRS = INNER // P
SUPPRESS = 20.0
BROWS = 6
SCORE_BANKS, TURN_BANKS = 4, 2
N_WDMA = 7


def build(nc, x, ctx, wq, wk, wv, wo, bo, norm_w, cols, idx, masks, ident, rowsel, iota, out):
    with ExitStack() as stack:
        def sb(name, shape, dt=F32):
            return stack.enter_context(nc.sbuf_tensor(name, shape, dt))

        def sem(name):
            return stack.enter_context(nc.semaphore(name))

        ps = stack.enter_context(nc.psum_tensor("ps", [P, 8, 512], F32))
        BANK_OUT, BANK_XT = 6, 7

        ident_sb = sb("ident_sb", [P, P])
        x_sb = sb("x_sb", [P, TILES, C])
        xres = sb("xres", [P, TILES, C])
        ctx_sb = sb("ctx_sb", [KEYS, BATCH, CTX])
        ctxT = sb("ctxT", [P, KC, BK])
        wq_sb = sb("wq_sb", [P, INNER])
        wk_sb = sb("wk_sb", [P, KC, INNER])
        wv_sb = sb("wv_sb", [P, KC, INNER])
        wo_sb = sb("wo_sb", [P, PAIRS, C])
        bo_sb = sb("bo_sb", [P, C])
        nw_sb = sb("nw_sb", [P, 1])
        cols_sb = sb("cols_sb", [P, 3])
        rowscale = sb("rowscale", [P, 1])
        wqs = sb("wqs", [P, INNER])
        wqT = sb("wqT", [P, PAIRS, C])
        kT = sb("kT", [P, 2, BK])
        vT = sb("vT", [P, 2, BK])
        m_hi = sb("m_hi", [P, BATCH, HEADS, KEYS], F32R)
        m_lo = sb("m_lo", [P, BATCH, HEADS, KEYS], F32R)
        vwT = sb("vwT", [P, BATCH, HEADS, KEYS])
        vw = sb("vw", [P, BATCH, len(CHUNKS), C])
        xT_hi = sb("xT_hi", [P, 2, P], F32R)
        xT_lo = sb("xT_lo", [P, 2, P], F32R)
        prob = sb("prob", [P, TPB, HK])
        mx = sb("mx", [P, TPB, HEADS])
        tot = sb("tot", [P, TPB, HEADS])
        rec = sb("rec", [P, TPB, HEADS])
        pT = sb("pT", [P, 2, len(CHUNKS), P])
        sq = sb("sq", [P, C])
        ssum = sb("ssum", [P, TILES])
        msum = sb("msum", [P, TILES])
        inv = sb("inv", [P, TILES])
        halfs = sb("halfs", [P, TILES])
        mask_sb = sb("mask_sb", [BROWS, SEQ])
        bias_r = sb("bias_r", [BROWS, SEQ])
        bias_s = sb("bias_s", [BROWS, SEQ])
        bias_p = sb("bias_p", [BROWS, 3, SEQ], BF16)
        bias_t = sb("bias_t", [BROWS, SEQ])
        bias_rows = sb("bias_rows", [BROWS, SEQ], BF16)
        rowsel_sb = sb("rowsel_sb", [BROWS, 3])
        iota_sb = sb("iota_sb", [BROWS, 2, KEYS])
        idx_sb = sb("idx_sb", [BROWS, LAYERS, 4], I32)
        idx_f = sb("idx_f", [BROWS, LAYERS, 4])
        hit = sb("hit", [BROWS, 8, LAYERS, KEYS])
        ind = sb("ind", [BROWS, LAYERS, KEYS])
        ind_rows = sb("ind_rows", [BROWS, HEADS, KEYS], BF16)

        s_const = sem("s_const")
        s_weights = sem("s_weights")
        s_small = sem("s_small")
        s_xready = sem("s_xready")
        s_stored = sem("s_stored")
        s_setup = sem("s_setup")
        s_bias = sem("s_bias")
        s_half = sem("s_half")
        s_ctx_mm = sem("s_ctx_mm")
        s_ctxT = sem("s_ctxT")
        s_scale = sem("s_scale")
        s_wqs = sem("s_wqs")
        s_ind = sem("s_ind")
        s_wqT_mm = sem("s_wqT_mm")
        s_wqT_act = sem("s_wqT_act")
        s_wqT_dve = sem("s_wqT_dve")
        s_k_mm, s_k = sem("s_k_mm"), sem("s_k")
        s_v_mm, s_v = sem("s_v_mm"), sem("s_v")
        s_m_mm, s_mhi, s_mlo = sem("s_m_mm"), sem("s_mhi"), sem("s_mlo")
        s_w_mm, s_w_act, s_w_dve = sem("s_w_mm"), sem("s_w_act"), sem("s_w_dve")
        s_vw_mm, s_vw_act, s_vw_dve = sem("s_vw_mm"), sem("s_vw_act"), sem("s_vw_dve")
        s_sumsq = sem("s_sumsq")
        s_msum = sem("s_msum")
        s_inv = sem("s_inv")
        s_xT_mm, s_xhi, s_xlo = sem("s_xT_mm"), sem("s_xhi"), sem("s_xlo")
        s_scores = sem("s_scores")
        s_max = sem("s_max")
        s_shift = sem("s_shift")
        s_exp = sem("s_exp")
        s_sum = sem("s_sum")
        s_rec = sem("s_rec")
        s_prob = sem("s_prob")
        s_pT_mm, s_pT = sem("s_pT_mm"), sem("s_pT")
        s_out = sem("s_out")
        s_res = sem("s_res")

        x_dram = x.rearrange("b (t p) c -> p (b t) c", p=P)
        out_dram = out.rearrange("b (t p) c -> p (b t) c", p=P)

        block = stack.enter_context(nc.Block())

        def by_head(ap):
            return ap.rearrange("p (h k) -> p h k", k=KEYS)

        def tile_steps(step, stages):
            for stage, ahead in stages:
                if 0 <= step + ahead < TILES:
                    stage(step + ahead)

        STEPS = range(-3, TILES + 2)

        @block.sync
        def _(sp):
            for dst, src in ((ident_sb[:], ident), (ctx_sb[:], ctx.rearrange("b k d -> k b d")),
                             (mask_sb[:], masks), (rowsel_sb[:], rowsel),
                             (iota_sb[:], iota), (idx_sb[:], idx)):
                sp.dma_start(dst, src).then_inc(s_const, 16)
            for l in range(LAYERS):
                if l >= 1:
                    sp.wait_ge(s_wqs, l)
                    sp.wait_ge(s_res, l * TILES)
                    sp.wait_ge(s_msum, l)
                sp.dma_start(nw_sb[:], norm_w[l]).then_inc(s_small, 16)
                sp.dma_start(cols_sb[:], cols[l]).then_inc(s_small, 16)
                sp.dma_start(bo_sb[:], bo[l]).then_inc(s_small, 16)
                if l >= 1:
                    sp.wait_ge(s_w_mm, l * HEADS)
                sp.dma_start(wq_sb[:], wq[l]).then_inc(s_weights, 16)
                wk_l = wk[l].rearrange("(k p) n -> p k n", p=P)
                wv_l = wv[l].rearrange("(k p) n -> p k n", p=P)
                sp.dma_start(wk_sb[:, 0], wk_l[:, 0]).then_inc(s_weights, 16)
                sp.dma_start(wk_sb[:, 1], wk_l[:, 1]).then_inc(s_weights, 16)
                sp.dma_start(wv_sb[:, 0], wv_l[:, 0]).then_inc(s_weights, 16)
                sp.dma_start(wv_sb[:, 1], wv_l[:, 1]).then_inc(s_weights, 16)
                wo_l = wo[l].rearrange("(c p) n -> p c n", p=P)
                sp.dma_start(wo_sb[:, 0:4], wo_l[:, 0:4]).then_inc(s_weights, 16)
                sp.dma_start(wo_sb[:, 4:8], wo_l[:, 4:8]).then_inc(s_weights, 16)
            for b in range(BATCH):
                sp.wait_ge(s_xready, LAYERS * TILES + TPB * (b + 1))
                sp.dma_start(out_dram[:, TPB * b:TPB * (b + 1)], x_sb[:, TPB * b:TPB * (b + 1)]).then_inc(s_stored, 16)
            sp.wait_ge(s_stored, 16 * BATCH)

        @block.tensor
        def _(pe):
            pe.wait_ge(s_const, 16 * 6)
            for kc in range(KC):
                for b in range(BATCH):
                    mm = nc.tensor.transpose(ps[:, kc, b * KEYS:(b + 1) * KEYS],
                                             ctx_sb[:, b, kc * P:(kc + 1) * P], ident_sb[0:KEYS, 0:KEYS])
                mm.then_inc(s_ctx_mm, 1)
            pe.wait_ge(s_ctxT, KC)

            with pe.Fori(0, LAYERS) as l:
                pe.wait_ge(s_xready, l * TILES + TILES)
                pe.wait_ge(s_wqs, l + 1)
                for half in range(2):
                    for i in range(4):
                        c = 4 * half + i
                        mm = nc.tensor.transpose(ps[:, 6 + half, i * P:(i + 1) * P], wqs[:, c * P:(c + 1) * P],
                                                 ident_sb[:])
                    mm.then_inc(s_wqT_mm, 1)
                pe.wait_ge(s_weights, (l + 1) * (16 * N_WDMA))

                def pair_k_v(c):
                    if c >= 1:
                        pe.wait_ge(s_k, l * PAIRS + c)
                    for kc in range(KC):
                        mm = nc.tensor.matmul(ps[:, 0, 0:BK], wk_sb[:, kc, c * P:(c + 1) * P], ctxT[:, kc],
                                              start=(kc == 0), stop=(kc == KC - 1))
                    mm.then_inc(s_k_mm, 1)
                    if c >= 1:
                        pe.wait_ge(s_v, l * PAIRS + c)
                    for kc in range(KC):
                        mm = nc.tensor.matmul(ps[:, 1, 0:BK], wv_sb[:, kc, c * P:(c + 1) * P], ctxT[:, kc],
                                              start=(kc == 0), stop=(kc == KC - 1))
                    mm.then_inc(s_v_mm, 1)

                def head_products(c):
                    pe.wait_ge(s_k, l * PAIRS + (c + 1))
                    for h in (2 * c, 2 * c + 1):
                        r = HDIM * (h % 2)
                        if h >= 2:
                            pe.wait_ge(s_mlo, l * HEADS + (h - 1))
                        nc.tensor.matmul(ps[:, 2 + h % 2, 0:BK], wqT[r:r + HDIM, c], kT[r:r + HDIM, c % 2],
                                         start=True, stop=True).then_inc(s_m_mm, 1)
                    pe.wait_ge(s_v, l * PAIRS + (c + 1))
                    for h in (2 * c, 2 * c + 1):
                        r = HDIM * (h % 2)
                        if h >= 2:
                            pe.wait_ge(s_w_act if h % 2 else s_w_dve, l * PAIRS + c)
                        nc.tensor.matmul(ps[:, 4 + h % 2, 0:BK], wo_sb[r:r + HDIM, c], vT[r:r + HDIM, c % 2],
                                         start=True, stop=True).then_inc(s_w_mm, 1)

                pair_k_v(0)
                pe.wait_ge(s_wqT_act, l + 1)
                pe.wait_ge(s_wqT_dve, l + 1)
                for c in range(PAIRS):
                    if c + 1 < PAIRS:
                        pair_k_v(c + 1)
                    head_products(c)

                pe.wait_ge(s_w_act, l * PAIRS + PAIRS)
                pe.wait_ge(s_w_dve, l * PAIRS + PAIRS)
                for b in range(BATCH):
                    flat = vwT[:, b].rearrange("p h k -> p (h k)")
                    for q, quad in enumerate(QUADS):
                        f = NQ * b + q
                        if f == 2:
                            pe.wait_ge(s_mlo, l * HEADS + HEADS)
                        if f >= 4:
                            pe.wait_ge(s_vw_dve if f % 2 else s_vw_act, l * 6 + (f // 2 - 1))
                        for i, (at, n) in enumerate(quad):
                            mm = nc.tensor.transpose(ps[0:n, f % 4, i * P:(i + 1) * P], flat[:, at:at + n], ident_sb[:])
                        mm.then_inc(s_vw_mm, 1)

                def turn_x(t):
                    if t >= 1:
                        pe.wait_ge(s_xlo, l * TILES + t)
                    nc.tensor.transpose(ps[:, BANK_XT, 0:P], x_sb[:, t], ident_sb[:]).then_inc(s_xT_mm, 1)

                def scores(t):
                    pe.wait_ge(s_xlo, l * TILES + (t + 1))
                    if t == 0:
                        pe.wait_ge(s_vw_act, l * 6 + 6)
                        pe.wait_ge(s_vw_dve, l * 6 + 6)
                        pe.wait_ge(s_ind, l + 1)
                    b = t // TPB
                    for g, (h0, nh) in enumerate(GROUPS):
                        n = NG * t + g
                        if n >= SCORE_BANKS:
                            pe.wait_ge(s_shift, l * (NG * TILES) + (n - SCORE_BANKS + 1))
                        bank = ps[:, n % SCORE_BANKS, 0:nh * KEYS]
                        hi = m_hi[:, b, h0:h0 + nh].rearrange("p h k -> p (h k)")
                        lo = m_lo[:, b, h0:h0 + nh].rearrange("p h k -> p (h k)")
                        at = (t % TPB) * P
                        nc.tensor.matmul(bank, xT_hi[:, t % 2], hi, start=True, stop=False)
                        nc.tensor.matmul(bank, xT_hi[:, t % 2], lo, start=False, stop=False)
                        nc.tensor.matmul(bank, xT_lo[:, t % 2], hi, start=False, stop=False)
                        nc.tensor.matmul(bank, bias_rows[:, at:at + P],
                                         ind_rows[:, h0:h0 + nh].rearrange("p h k -> p (h k)"),
                                         start=False, stop=True).then_inc(s_scores, 1)

                def turn_probs(t):
                    pe.wait_ge(s_prob, l * TILES + (t + 1))
                    for q, quad in enumerate(QUADS):
                        n = NQ * t + q
                        if n >= TURN_BANKS:
                            pe.wait_ge(s_pT, l * (NQ * TILES) + (n - TURN_BANKS + 1))
                        for i, (at, rows) in enumerate(quad):
                            mm = nc.tensor.transpose(ps[0:rows, 4 + n % TURN_BANKS, i * P:(i + 1) * P],
                                                     prob[:, t % TPB, at:at + rows], ident_sb[:])
                        mm.then_inc(s_pT_mm, 1)

                def output(t):
                    pe.wait_ge(s_pT, l * (NQ * TILES) + NQ * (t + 1))
                    if t >= 1:
                        pe.wait_ge(s_xready, l * TILES + (TILES + t))
                    for c, (at, rows) in enumerate(CHUNKS):
                        mm = nc.tensor.matmul(ps[:, BANK_OUT, 0:C], pT[0:rows, t % 2, c], vw[0:rows, t // TPB, c],
                                              start=(c == 0), stop=(c == len(CHUNKS) - 1))
                    mm.then_inc(s_out, 1)

                for step in STEPS:
                    tile_steps(step, ((turn_x, 3), (scores, 2), (turn_probs, 0), (output, -1)))

        @block.scalar
        def _(act):
            act.dma_start(x_sb[:], x_dram).then_inc(s_xready, 16)
            act.wait_ge(s_ctx_mm, 1)
            nc.scalar.copy(ctxT[:, 0], ps[:, 0, 0:BK]).then_inc(s_ctxT, 1)

            with act.Fori(0, LAYERS) as l:
                act.wait_ge(s_wqT_mm, l * 2 + 1)
                nc.scalar.copy(wqT[:, 0:4].rearrange("p c n -> p (c n)"), ps[:, 6]).then_inc(s_wqT_act, 1)

                def keep_k(c):
                    act.wait_ge(s_k_mm, l * PAIRS + (c + 1))
                    if c >= 2:
                        act.wait_ge(s_m_mm, l * HEADS + 2 * (c - 1))
                    nc.scalar.copy(kT[:, c % 2], ps[:, 0, 0:BK]).then_inc(s_k, 1)

                keep_k(0)
                for c in range(PAIRS):
                    if c + 1 < PAIRS:
                        keep_k(c + 1)
                    for h in (2 * c, 2 * c + 1):
                        act.wait_ge(s_m_mm, l * HEADS + (h + 1))
                        nc.scalar.copy(m_hi[:, :, h], ps[:, 2 + h % 2, 0:BK].rearrange("p (b k) -> p b k", k=KEYS)
                                       ).then_inc(s_mhi, 1)
                    h = 2 * c + 1
                    act.wait_ge(s_w_mm, l * HEADS + (h + 1))
                    nc.scalar.copy(vwT[:, :, h], ps[:, 5, 0:BK].rearrange("p (b k) -> p b k", k=KEYS)).then_inc(s_w_act, 1)
                for f in range(0, NQ * BATCH, 2):
                    act.wait_ge(s_vw_mm, l * (NQ * BATCH) + (f + 1))
                    copy_quad(nc.scalar.copy, vw[:, f // NQ], f % NQ, ps[:, f % 4]).then_inc(s_vw_act, 1)

                def keep_x_hi(t):
                    act.wait_ge(s_xT_mm, l * TILES + (t + 1))
                    if t >= 2:
                        act.wait_ge(s_scores, l * (NG * TILES) + NG * (t - 1))
                    nc.scalar.copy(xT_hi[:, t % 2], ps[:, BANK_XT, 0:P]).then_inc(s_xhi, 1)

                def exp(t):
                    if t == 0:
                        act.wait_ge(s_inv, l + 1)
                    act.wait_ge(s_shift, l * (NG * TILES) + NG * (t + 1))
                    nc.scalar.activation(prob[:, t % TPB], prob[:, t % TPB], ACT.Exp, scale=inv[:, t:t + 1]
                                         ).then_inc(s_exp, 1)

                def keep_pT(t):
                    for q in range(NQ):
                        n = NQ * t + q
                        act.wait_ge(s_pT_mm, l * (NQ * TILES) + (n + 1))
                        if q == 0 and t >= 2:
                            act.wait_ge(s_out, l * TILES + (t - 1))
                        copy_quad(nc.scalar.copy, pT[:, t % 2], q, ps[:, 4 + n % TURN_BANKS]).then_inc(s_pT, 1)

                for step in STEPS:
                    tile_steps(step, ((keep_x_hi, 3), (exp, 1), (keep_pT, 0)))

        @block.vector
        def _(dve):
            done = [0]

            def chain(ins):
                done[0] += 1
                ins.then_inc(s_setup, 1)
                dve.wait_ge(s_setup, done[0])

            dve.wait_ge(s_const, 16 * 6)
            chain(nc.vector.tensor_scalar(bias_r[:], mask_sb[:], 1.0, SUPPRESS, ALU.subtract, ALU.mult))
            chain(nc.vector.tensor_copy(bias_p[:, 0], bias_r[:]))
            chain(nc.vector.tensor_tensor(bias_s[:], bias_r[:], bias_p[:, 0], ALU.subtract))
            chain(nc.vector.tensor_copy(bias_p[:, 1], bias_s[:]))
            chain(nc.vector.tensor_tensor(bias_r[:], bias_s[:], bias_p[:, 1], ALU.subtract))
            chain(nc.vector.tensor_copy(bias_p[:, 2], bias_r[:]))
            chain(nc.vector.tensor_scalar(bias_t[:], bias_p[:, 0], rowsel_sb[:, 0:1], None, ALU.mult))
            chain(nc.vector.scalar_tensor_tensor(bias_s[:], bias_p[:, 1], rowsel_sb[:, 1:2], bias_t[:], ALU.mult, ALU.add))
            nc.vector.scalar_tensor_tensor(bias_rows[:], bias_p[:, 2], rowsel_sb[:, 2:3], bias_s[:],
                                           ALU.mult, ALU.add).then_inc(s_bias, 1)
            chain(nc.vector.tensor_copy(idx_f[:], idx_sb[:]))
            for j in range(4):
                for w in range(2):
                    last = nc.vector.tensor_tensor(hit[:, 2 * j + w],
                                                   iota_sb[:, w].unsqueeze(1).to_broadcast([BROWS, LAYERS, KEYS]),
                                                   idx_f[:, :, j:j + 1].to_broadcast([BROWS, LAYERS, KEYS]), ALU.is_equal)
            chain(last)
            chain(nc.vector.tensor_tensor(hit[:, 0:2], hit[:, 0:2], hit[:, 2:4], ALU.max))
            chain(nc.vector.tensor_tensor(hit[:, 4:6], hit[:, 4:6], hit[:, 6:8], ALU.max))
            chain(nc.vector.tensor_tensor(hit[:, 0], hit[:, 0], hit[:, 1], ALU.max))
            chain(nc.vector.tensor_tensor(hit[:, 4], hit[:, 4], hit[:, 5], ALU.max))
            chain(nc.vector.tensor_scalar(hit[:, 5], hit[:, 4], -1.0, 1.0, ALU.mult, ALU.add))
            chain(nc.vector.tensor_tensor(ind[:], hit[:, 0], hit[:, 5], ALU.mult))
            nc.vector.memset(halfs[:], -0.5).then_inc(s_half, 1)
            dve.wait_ge(s_ctx_mm, 2)
            nc.vector.tensor_copy(ctxT[:, 1], ps[:, 1, 0:BK]).then_inc(s_ctxT, 1)

            with dve.Fori(0, LAYERS) as l:
                dve.wait_ge(s_small, (l + 1) * 48)
                dve.wait_ge(s_xready, l * TILES + TILES)
                nc.vector.tensor_tensor(rowscale[:], nw_sb[:], cols_sb[:, 0:1], ALU.mult).then_inc(s_scale, 1)
                dve.wait_ge(s_weights, (l + 1) * (16 * N_WDMA))
                dve.wait_ge(s_scale, l + 1)
                nc.vector.tensor_scalar(wqs[:], wq_sb[:], rowscale[:, 0:1], None, ALU.mult).then_inc(s_wqs, 1)
                nc.vector.tensor_copy(ind_rows[:], ind[:, bass.ds(l, 1)].to_broadcast([BROWS, HEADS, KEYS])
                                      ).then_inc(s_ind, 1)
                for t in range(TILES):
                    if t >= 1:
                        dve.wait_ge(s_sumsq, l * TILES + t)
                    nc.vector.tensor_tensor_reduce(sq[:], x_sb[:, t], x_sb[:, t], 1.0, 0.0, ALU.mult, ALU.add,
                                                   ssum[:, t:t + 1]).then_inc(s_sumsq, 1)
                dve.wait_ge(s_sumsq, l * TILES + TILES)
                nc.vector.tensor_scalar(msum[:], ssum[:], cols_sb[:, 1:2], cols_sb[:, 2:3], ALU.mult, ALU.add
                                        ).then_inc(s_msum, 1)

                dve.wait_ge(s_wqT_mm, l * 2 + 2)
                nc.vector.tensor_copy(wqT[:, 4:8].rearrange("p c n -> p (c n)"), ps[:, 7]).then_inc(s_wqT_dve, 1)

                def keep_v(c):
                    dve.wait_ge(s_v_mm, l * PAIRS + (c + 1))
                    if c >= 2:
                        dve.wait_ge(s_w_mm, l * HEADS + 2 * (c - 1))
                    nc.vector.tensor_copy(vT[:, c % 2], ps[:, 1, 0:BK]).then_inc(s_v, 1)

                keep_v(0)
                for c in range(PAIRS):
                    if c + 1 < PAIRS:
                        keep_v(c + 1)
                    for h in (2 * c, 2 * c + 1):
                        dve.wait_ge(s_mhi, l * HEADS + (h + 1))
                        nc.vector.tensor_tensor(m_lo[:, :, h], ps[:, 2 + h % 2, 0:BK].rearrange("p (b k) -> p b k", k=KEYS),
                                                m_hi[:, :, h].bitcast(F32), ALU.subtract).then_inc(s_mlo, 1)
                    h = 2 * c
                    dve.wait_ge(s_w_mm, l * HEADS + (h + 1))
                    nc.vector.tensor_copy(vwT[:, :, h], ps[:, 4, 0:BK].rearrange("p (b k) -> p b k", k=KEYS)
                                          ).then_inc(s_w_dve, 1)
                for f in range(1, NQ * BATCH, 2):
                    dve.wait_ge(s_vw_mm, l * (NQ * BATCH) + (f + 1))
                    copy_quad(nc.vector.tensor_copy, vw[:, f // NQ], f % NQ, ps[:, f % 4]).then_inc(s_vw_dve, 1)

                def add_residual(t):
                    dve.wait_ge(s_out, l * TILES + (t + 1))
                    dve.wait_ge(s_res, l * TILES + (t + 1))
                    nc.vector.tensor_tensor(x_sb[:, t], ps[:, BANK_OUT, 0:C], xres[:, t], ALU.add).then_inc(s_xready, 1)

                def keep_x_lo(t):
                    dve.wait_ge(s_xhi, l * TILES + (t + 1))
                    if t >= 2:
                        dve.wait_ge(s_scores, l * (NG * TILES) + NG * (t - 1))
                    nc.vector.tensor_tensor(xT_lo[:, t % 2], ps[:, BANK_XT, 0:P], xT_hi[:, t % 2].bitcast(F32),
                                            ALU.subtract).then_inc(s_xlo, 1)

                def shift(t):
                    for g, (h0, nh) in enumerate(GROUPS):
                        n = NG * t + g
                        bank = by_head(ps[:, n % SCORE_BANKS, 0:nh * KEYS])
                        dve.wait_ge(s_scores, l * (NG * TILES) + (n + 1))
                        nc.vector.tensor_reduce(mx[:, t % TPB, h0:h0 + nh], bank, AX.X, ALU.max).then_inc(s_max, 1)
                        if g == 0 and t >= TPB:
                            dve.wait_ge(s_pT_mm, l * (NQ * TILES) + NQ * (t - TPB + 1))
                        dve.wait_ge(s_max, l * (NG * TILES) + (n + 1))
                        nc.vector.tensor_tensor(by_head(prob[:, t % TPB, h0 * KEYS:(h0 + nh) * KEYS]), bank,
                                                mx[:, t % TPB, h0:h0 + nh].unsqueeze(2).to_broadcast([P, nh, KEYS]),
                                                ALU.subtract).then_inc(s_shift, 1)

                def denominators(t):
                    dve.wait_ge(s_exp, l * TILES + (t + 1))
                    nc.vector.tensor_reduce(tot[:, t % TPB], by_head(prob[:, t % TPB]), AX.X, ALU.add).then_inc(s_sum, 1)
                    dve.wait_ge(s_sum, l * TILES + (t + 1))
                    nc.vector.reciprocal(rec[:, t % TPB], tot[:, t % TPB]).then_inc(s_rec, 1)

                for step in STEPS:
                    tile_steps(step, ((add_residual, -2), (keep_x_lo, 3), (shift, 2), (denominators, 1)))

        @block.gpsimd
        def _(pool):
            pool.wait_ge(s_half, 1)
            with pool.Fori(0, LAYERS) as l:
                pool.wait_ge(s_small, (l + 1) * 48)
                pool.wait_ge(s_msum, l + 1)
                nc.gpsimd.tensor_tensor(inv[:], msum[:], halfs[:], ALU.pow).then_inc(s_inv, 1)
                pool.wait_ge(s_xready, l * TILES + TILES)
                for t in range(TILES):
                    nc.gpsimd.tensor_tensor(xres[:, t], x_sb[:, t], bo_sb[:], ALU.add).then_inc(s_res, 1)

                for t in range(TILES):
                    pool.wait_ge(s_rec, l * TILES + (t + 1))
                    nc.gpsimd.tensor_tensor(by_head(prob[:, t % TPB]), by_head(prob[:, t % TPB]),
                                            rec[:, t % TPB].unsqueeze(2).to_broadcast([P, HEADS, KEYS]),
                                            ALU.mult).then_inc(s_prob, 1)


def copy_quad(copy, dst, q, bank):
    full = [c for c in range(4 * q, min(4 * q + 4, len(CHUNKS))) if CHUNKS[c][1] == P]
    last = copy(dst[:, full[0]:full[-1] + 1].rearrange("p c n -> p (c n)"), bank[:, 0:len(full) * P])
    for c in range(4 * q + len(full), min(4 * q + 4, len(CHUNKS))):
        rows, at = CHUNKS[c][1], (c - 4 * q) * P
        last = copy(dst[0:rows, c], bank[0:rows, at:at + P])
    return last


def lay_out(inputs):
    import numpy as np

    def heads64(w, axis):
        shape = list(w.shape)
        shape[axis:axis + 1] = [HEADS, HDIM]
        full = np.zeros(shape, w.dtype)
        small = list(w.shape)
        small[axis:axis + 1] = [HEADS, w.shape[axis] // HEADS]
        at = [slice(None)] * len(shape)
        at[axis + 1] = slice(0, w.shape[axis] // HEADS)
        full[tuple(at)] = w.reshape(small)
        shape = list(w.shape)
        shape[axis] = INNER
        return full.reshape(shape)

    def repeated(w):
        kv = 4
        d = w.shape[1] // kv
        return np.repeat(w.reshape(w.shape[0], kv, d), HEADS // kv, axis=1).reshape(w.shape[0], HEADS * d)

    big = ("L0_xattn_", "L2_xattn_", "L3_xattn_")
    a = {k: np.asarray(v) for k, v in inputs.items()}

    def stack(name, one):
        return np.stack([a[big[0] + name], one, a[big[1] + name], a[big[2] + name]])

    d = {"x": a["x"], "ctx": a["ctx_2048"]}
    d["wq"] = stack("Wq", heads64(a["L1_xattn_wq"], 1))
    d["wk"] = stack("Wk", heads64(repeated(a["L1_xattn_wk"]), 1))
    d["wv"] = stack("Wv", heads64(repeated(a["L1_xattn_wv"]), 1))
    d["wo"] = stack("Wo", heads64(a["L1_xattn_wo"], 0))
    zeros, ones = np.zeros((C,), np.float32), np.ones((C,), np.float32)
    bo = stack("bo", zeros)
    d["bo"] = np.ascontiguousarray(np.broadcast_to(bo[:, None, :], (LAYERS, P, C)))
    d["norm_w"] = np.stack([ones, a["L1_xattn_norm_w"], ones, ones]).reshape(LAYERS, P, 1)
    plain, normed = (HDIM ** -0.5, 0.0, 1.0), (8 ** -0.5, 1.0 / C, 1e-5)
    cols = np.array([plain, normed, plain, plain], np.float32)
    d["cols"] = np.ascontiguousarray(np.broadcast_to(cols[:, None, :], (LAYERS, P, 3)))
    none = np.full((2,), -1000, np.int32)
    rows = np.zeros((BROWS, LAYERS, 4), np.int32)
    for l, name in enumerate(("L0_xattn_", None, "L2_xattn_", "L3_xattn_")):
        first = a[name + "token_indices_A"] if name else none
        second = a[name + "token_indices_B"] if name else none
        rows[0:3, l] = np.concatenate([first, second])
        rows[3:6, l] = np.concatenate([second, none])
    d["idx"] = rows
    d["masks"] = np.repeat(np.stack([a["mask_S_fk1"], a["mask_S_fk0"]]), 3, axis=0)
    d["ident"] = np.eye(P, dtype=np.float32)
    d["rowsel"] = np.tile(np.eye(3, dtype=np.float32), (2, 1))
    iota = np.arange(KEYS, dtype=np.float32)
    d["iota"] = np.ascontiguousarray(np.broadcast_to(np.stack([iota, iota - KEYS]), (BROWS, 2, KEYS)))
    return d


def kernel(**inputs):
    import numpy as np
    import concourse.bacc as bacc
    from concourse.bass_utils import run_bass_kernel_spmd

    nc = bacc.Bacc("TRN2", target_bir_lowering=False, num_devices=1)
    arrays, aps = {}, {}
    for name, value in lay_out(inputs).items():
        value = np.ascontiguousarray(value)
        arrays[f"in_{name}"] = value
        aps[name] = nc.dram_tensor(f"in_{name}", value.shape, mybir.dt.from_np(value.dtype), kind="ExternalInput").ap()
    out = nc.dram_tensor("out_x", (BATCH, SEQ, C), F32, kind="ExternalOutput").ap()
    build(nc, out=out, **aps)
    result = run_bass_kernel_spmd(nc, [arrays], core_ids=[0])
    return result.results[0]["out_x"]
```

```python
from contextlib import ExitStack

import concourse.bass as bass
from concourse import mybir

F32 = mybir.dt.float32
F32R = mybir.dt.float32r
I32 = mybir.dt.int32
ALU = mybir.AluOpType
ACT = mybir.ActivationFunctionType
AX = mybir.AxisListType

LAYERS = 4
BATCH, SEQ, C = 4, 512, 128
KEYS, CTX = 77, 256
HEADS, HDIM = 16, 64
INNER = HEADS * HDIM
P = 128
TILES = BATCH * SEQ // P
TPB = SEQ // P
HK = HEADS * KEYS
BK = BATCH * KEYS
CHUNKS = [(c * P, min(P, HK - c * P)) for c in range((HK + P - 1) // P)]
QUADS = [CHUNKS[0:4], CHUNKS[4:8], CHUNKS[8:10]]
NQ = len(QUADS)
HPB = 4
HALF = 2 * HPB
OUT_PARTS = [(0, 3), (3, 6), (6, 8), (8, 10)]
KC = CTX // P
PAIRS = INNER // P
SUPPRESS = 20.0
RING = 4
MARKED = 4
NORM_W, SCALE, MEAN, EPS, BO = range(5)

TURN_BANK, OUT_BANK = 4, 7


def now(*steps):
    return [(step, n, 0) for step, n in steps]


def ahead(*steps):
    return [(step, n, 1) for step, n in steps]


def tile_step(s, *beside):
    steps = [("scores", s + 3)] if s + 3 < TILES else []
    steps += [("normalise", s + 1)] if 0 <= s + 1 < TILES else []
    steps += [("shift", s + 3)] if s + 3 < TILES else []
    steps += [("exp", s + 2)] if 0 <= s + 2 < TILES else []
    steps += [("residual", s // TPB - 2)] if s >= 8 and s % TPB == 0 else []
    steps += list(beside)
    steps += [("turn", s)] if s >= 0 else []
    steps += [("output", s - TPB)] if s >= TPB else []
    steps += [("split", s // TPB - 2)] if s >= 8 and s % TPB == 1 else []
    return steps


REST = ahead(*tile_step(-3, ("norm", 0), ("w", 0), ("w", 1)), *tile_step(-2, ("w", 2), ("w", 3), ("w", 4)),
             *tile_step(-1, ("w", 5), ("w", 6), ("w", 7)))
FIRST = (ahead(("scale", 0), ("turn_w", 0), ("kv", 0), ("kv", 1), ("m", 0))
         + [x for c in range(1, PAIRS)
            for x in (ahead(("kv", c + 1)) if c < PAIRS - 1 else []) + ahead(("m", c))
            + (ahead(("turn_x", c - 3)) if 3 <= c < 3 + BATCH else [])]
         + REST)
TILE_STEPS = [x for s in range(13) for x in tile_step(s, *([("vw", s)] if s < BATCH else []))]
LAYER = (
    now(*TILE_STEPS) + ahead(("scale", 0)) + now(*tile_step(13)) + ahead(("turn_w", 0))
    + now(*tile_step(14)) + ahead(("kv", 0)) + now(*tile_step(15)) + ahead(("kv", 1))
    + now(("residual", 2)) + ahead(("m", 0), ("kv", 2)) + now(("output", 12)) + ahead(("m", 1), ("kv", 3))
    + now(("split", 2), ("output", 13)) + ahead(("m", 2), ("kv", 4)) + now(("output", 14))
    + ahead(("m", 3), ("kv", 5)) + now(("output", 15)) + ahead(("m", 4), ("kv", 6))
    + now(("residual", 3)) + ahead(("m", 5), ("kv", 7)) + now(("split", 3)) + ahead(("m", 6), ("m", 7)) + REST)
LAST = now(*[x for x in TILE_STEPS if x[0] != "split"]) + now(
    *[x for s in (13, 14, 15) for x in tile_step(s) if x[0] != "split"],
    ("residual", 2), ("final", 0), ("output", 12), ("output", 13), ("final", 1), ("output", 14), ("final", 2),
    ("output", 15), ("residual", 3), ("final", 3))


def build(nc, x, ctx, wq, wk, wv, wo, vectors, idx, ranks, out):
    with ExitStack() as stack:
        def sb(name, shape, dt=F32):
            return stack.enter_context(nc.sbuf_tensor(name, shape, dt))

        def sem(name):
            return stack.enter_context(nc.semaphore(name))

        ps = stack.enter_context(nc.psum_tensor("ps", [P, 8, 512], F32))

        vectors_sb = sb("vectors_sb", [P, P + 5 * LAYERS + 2 * TPB])
        ident_sb = vectors_sb[:, 0:P]
        small_sb = vectors_sb[:, P:P + 5 * LAYERS].rearrange("p (l n) -> p l n", n=5)
        mask_sb = vectors_sb[:, P + 5 * LAYERS:].rearrange("p (s j) -> p s j", j=TPB)
        x_sb = sb("x_sb", [P, TILES, C])
        xsq = x_sb[:].rearrange("p (b j) c -> p b (j c)", b=BATCH)
        xT = sb("xT", [P, BATCH, SEQ])
        xT_hi = sb("xT_hi", [P, BATCH, SEQ], F32R)
        xT_lo = sb("xT_lo", [P, BATCH, SEQ], F32R)
        ones = sb("ones", [P, 1])
        halfs = sb("halfs", [P, TILES])
        msum = sb("msum", [P, TILES])
        inv = sb("inv", [P, TILES])
        bo_now = sb("bo_now", [P, 1])
        rowscale = sb("rowscale", [P, LAYERS])
        ctx_sb = sb("ctx_sb", [KEYS, BATCH, CTX])
        ctxT = sb("ctxT", [P, KC, BK])
        wq_sb = sb("wq_sb", [P, INNER])
        wk_sb = sb("wk_sb", [P, KC, INNER])
        wv_sb = sb("wv_sb", [P, KC, INNER])
        wo_sb = sb("wo_sb", [P, PAIRS, C])
        wqT = sb("wqT", [P, PAIRS, C])
        m_hi = sb("m_hi", [P, BATCH, HEADS, KEYS], F32R)
        m_lo = sb("m_lo", [P, BATCH, HEADS, KEYS], F32R)
        vwT = sb("vwT", [P, BATCH, HEADS, KEYS])
        kT = vwT[:, 0:2].rearrange("p b h k -> p (b h k)").rearrange("p (c n) -> p c n", n=BK)
        vw = sb("vw", [P, BATCH, len(CHUNKS), C])
        vT = vw[:, 0:2].rearrange("p b c n -> p (b c n)")[:, 0:PAIRS * BK].rearrange("p (c n) -> p c n", n=BK)
        prob = sb("prob", [P, RING, HK])
        mx = sb("mx", [P, RING, HEADS])
        tot = sb("tot", [P, RING, HEADS])
        rec = sb("rec", [P, RING, HEADS])
        pT = sb("pT", [P, 2, len(CHUNKS), SEQ])
        used = [0]

        def scratch(*shape):
            size = 1
            for n in shape:
                size *= n
            at = used[0]
            used[0] += size
            flat = pT[0:KEYS, 1].rearrange("p c n -> p (c n)")[:, at:at + size]
            if len(shape) == 1:
                return flat
            names = "abc"[:len(shape)]
            return flat.rearrange(f"p ({' '.join(names)}) -> p {' '.join(names)}", **dict(zip(names, shape)))

        side_bias = sb("side_bias", [P, 2, TPB])
        in_place = sb("in_place", [P, LAYERS, 2, MARKED])
        bias_a = sb("bias_a", [P, TPB, MARKED])
        bias = sb("bias", [P, TPB, MARKED])
        ranks_sb = scratch(2 + 3 * KEYS)
        key_sb = ranks_sb[:, 0:2]
        keys_sb = ranks_sb[:, 2:2 + KEYS]
        before_sb = ranks_sb[:, 2 + KEYS:2 + 2 * KEYS]
        upto_sb = ranks_sb[:, 2 + 2 * KEYS:]
        idx_sb = sb("idx_sb", [KEYS, LAYERS, 4], I32)
        idx_f = scratch(LAYERS, 4)
        hit = scratch(2, LAYERS, 4)
        in_b = scratch(LAYERS)
        not_b = scratch(LAYERS)
        in_a = scratch(LAYERS)
        marked = scratch(LAYERS)
        plain = scratch(LAYERS)
        slot = scratch(3, LAYERS)
        sides = scratch(LAYERS, 2, P)
        order = sb("order", [KEYS, LAYERS, KEYS])

        s_idx = sem("s_idx")
        s_const = sem("s_const")
        s_ctx = sem("s_ctx")
        s_x = sem("s_x")
        s_wq, s_wk, s_wv, s_wo = sem("s_wq"), sem("s_wk"), sem("s_wv"), sem("s_wo")
        s_stored = sem("s_stored")
        s_half = sem("s_half")
        s_setup = sem("s_setup")
        s_ready = sem("s_ready")
        s_marked = sem("s_marked")
        s_cum_mm = sem("s_cum_mm")
        s_order = sem("s_order")
        s_ind_mm = sem("s_ind_mm")
        s_ind = sem("s_ind")
        s_bias = sem("s_bias")
        s_biased = sem("s_biased")
        s_xT_mm, s_xT_act = sem("s_xT_mm"), sem("s_xT_act")
        s_xhi, s_xlo = sem("s_xhi"), sem("s_xlo")
        s_xsq = sem("s_xsq")
        s_norm_mm, s_msum, s_inv = sem("s_norm_mm"), sem("s_msum"), sem("s_inv")
        s_wqs = sem("s_wqs")
        s_wqT_mm, s_wqT_act, s_wqT_dve = sem("s_wqT_mm"), sem("s_wqT_act"), sem("s_wqT_dve")
        s_ctx_mm, s_ctx_act, s_ctx_dve = sem("s_ctx_mm"), sem("s_ctx_act"), sem("s_ctx_dve")
        s_k_mm, s_k = sem("s_k_mm"), sem("s_k")
        s_v_mm, s_v = sem("s_v_mm"), sem("s_v")
        s_m_mm, s_mhi, s_mlo = sem("s_m_mm"), sem("s_mhi"), sem("s_mlo")
        s_w_mm, s_w = sem("s_w_mm"), sem("s_w")
        s_vw_mm, s_vw = sem("s_vw_mm"), sem("s_vw")
        s_scores = sem("s_scores")
        s_max = sem("s_max")
        s_shift = sem("s_shift")
        s_exp, s_sum, s_rec, s_prob = sem("s_exp"), sem("s_sum"), sem("s_rec"), sem("s_prob")
        s_pT_mm, s_pT = sem("s_pT_mm"), sem("s_pT")
        s_out = sem("s_out")
        s_bo = sem("s_bo")
        s_biased_out = sem("s_biased_out")
        s_resid = sem("s_resid")
        s_fin_mm, s_fin = sem("s_fin_mm"), sem("s_fin")

        x_dram = x.rearrange("b (t p) c -> p (b t) c", p=P)
        out_dram = out.rearrange("b (t p) c -> p (b t) c", p=P)

        block = stack.enter_context(nc.Block())

        def by_head(ap):
            return ap.rearrange("p (h k) -> p h k", k=KEYS)

        def by_batch(bank):
            return bank[:, 0:BK].rearrange("p (b k) -> p b k", k=KEYS)

        def half_banks(h):
            return ps[:, 2 * h:2 * h + 2, 0:HPB * KEYS].rearrange("p a (h k) -> p a h k", k=KEYS)

        def walk(schedule, l, does):
            for step, n, later in schedule:
                if step in does:
                    does[step](l + later, n)

        def run(engine, does):
            walk(FIRST, -1, does)
            with engine.Fori(0, LAYERS - 1) as l:
                walk(LAYER, l, does)
            walk(LAST, LAYERS - 1, does)

        def first(l):
            return isinstance(l, int) and l == 0

        @block.sync
        def _(sp):
            for l in range(LAYERS):
                if l >= 1:
                    sp.wait_ge(s_wqT_mm, 2 * l)
                    sp.wait_ge(s_w_mm, l * HEADS)
                sp.dma_start(wq_sb[:], wq[l]).then_inc(s_wq, 16)
                sp.dma_start(wk_sb[:], wk[l].rearrange("(k p) n -> p k n", p=P)).then_inc(s_wk, 16)
                sp.dma_start(wv_sb[:], wv[l].rearrange("(k p) n -> p k n", p=P)).then_inc(s_wv, 16)
                if l == 0:
                    sp.dma_start(x_sb[:], x_dram).then_inc(s_x, 16)
                sp.dma_start(wo_sb[:], wo[l].rearrange("(c p) n -> p c n", p=P)).then_inc(s_wo, 16)
            for b in range(BATCH):
                sp.wait_ge(s_fin, b + 1)
                sp.dma_start(out_dram[:, TPB * b:TPB * (b + 1)], x_sb[:, TPB * b:TPB * (b + 1)]).then_inc(s_stored, 16)
            sp.wait_ge(s_stored, 16 * BATCH)

        @block.tensor
        def _(pe):
            pe.wait_ge(s_idx, 32)
            pe.wait_ge(s_marked, 1)
            nc.tensor.matmul(ps[0:KEYS, 4, 0:LAYERS], before_sb, marked, start=True, stop=True)
            nc.tensor.matmul(ps[0:KEYS, 4, LAYERS:2 * LAYERS], upto_sb, marked,
                             start=True, stop=True).then_inc(s_cum_mm, 1)
            pe.wait_ge(s_order, 1)
            for l in range(LAYERS):
                for side in range(2):
                    at = (2 * l + side) * MARKED
                    mm = nc.tensor.matmul(ps[:, 5, at:at + MARKED], sides[:, l, side], order[:, l, 0:MARKED],
                                          start=True, stop=True)
            mm.then_inc(s_ind_mm, 1)

            def turn_w(l, _):
                pe.wait_ge(s_wqs, l + 1)
                if first(l):
                    pe.wait_ge(s_const, 16)
                else:
                    pe.wait_ge(s_shift, l * (2 * TILES) - 1)
                for half in range(2):
                    for i in range(4):
                        c = 4 * half + i
                        mm = nc.tensor.transpose(ps[:, half, i * P:(i + 1) * P], wq_sb[:, c * P:(c + 1) * P], ident_sb)
                    mm.then_inc(s_wqT_mm, 1)
                if first(l):
                    pe.wait_ge(s_ctx, 16)
                else:
                    pe.wait_ge(s_shift, l * (2 * TILES))
                for kc in range(KC):
                    for b in range(BATCH):
                        mm = nc.tensor.matmul(ps[:, 2 + kc, b * KEYS:(b + 1) * KEYS], ctx_sb[:, b, kc * P:(kc + 1) * P],
                                              order[:, l], start=True, stop=True)
                    mm.then_inc(s_ctx_mm, 1)

            def turn_x(_, b):
                if b == 0:
                    pe.wait_ge(s_x, 16)
                    pe.wait_ge(s_ind, 1)
                for j in range(TPB):
                    mm = nc.tensor.transpose(ps[:, 4 + b, j * P:(j + 1) * P], x_sb[:, TPB * b + j], ident_sb)
                mm.then_inc(s_xT_mm, 1)

            def kv(l, c):
                if c == 0:
                    pe.wait_ge(s_wk, (l + 1) * 16)
                    pe.wait_ge(s_ctx_act, l + 1)
                    pe.wait_ge(s_ctx_dve, l + 1)
                    pe.wait_ge(s_wqT_act, l + 1)
                    pe.wait_ge(s_wqT_dve, l + 1)
                else:
                    pe.wait_ge(s_k, l * PAIRS + c)
                for kc in range(KC):
                    mm = nc.tensor.matmul(ps[:, 0, 0:BK], wk_sb[:, kc, c * P:(c + 1) * P], ctxT[:, kc],
                                          start=(kc == 0), stop=(kc == KC - 1))
                mm.then_inc(s_k_mm, 1)
                if c == 0:
                    pe.wait_ge(s_wv, (l + 1) * 16)
                else:
                    pe.wait_ge(s_v, l * PAIRS + c)
                for kc in range(KC):
                    mm = nc.tensor.matmul(ps[:, 1, 0:BK], wv_sb[:, kc, c * P:(c + 1) * P], ctxT[:, kc],
                                          start=(kc == 0), stop=(kc == KC - 1))
                mm.then_inc(s_v_mm, 1)

            def m(l, c):
                pe.wait_ge(s_k, l * PAIRS + (c + 1))
                for h in (2 * c, 2 * c + 1):
                    r = HDIM * (h % 2)
                    if h >= 2:
                        pe.wait_ge(s_mlo, l * HEADS + (h - 1))
                    nc.tensor.matmul(ps[:, 2 + h % 2, 0:BK], wqT[r:r + HDIM, c], kT[r:r + HDIM, c],
                                     start=True, stop=True).then_inc(s_m_mm, 1)

            def w(l, c):
                if c == 0:
                    pe.wait_ge(s_wo, (l + 1) * 16)
                    pe.wait_ge(s_v, l * PAIRS + PAIRS)
                    if first(l):
                        pe.wait_ge(s_xT_act, 4)
                for h in (2 * c, 2 * c + 1):
                    r = HDIM * (h % 2)
                    if h >= 3:
                        pe.wait_ge(s_w, l * HEADS + (h - 2))
                    nc.tensor.matmul(ps[:, TURN_BANK + h % 3, 0:BK], wo_sb[r:r + HDIM, c], vT[r:r + HDIM, c],
                                     start=True, stop=True).then_inc(s_w_mm, 1)

            def norm(l, _):
                pe.wait_ge(s_xsq, (l + 1) * BATCH)
                for t in range(TILES):
                    mm = nc.tensor.matmul(ps[:, OUT_BANK, t:t + 1], xsq[:, t // TPB, (t % TPB) * P:(t % TPB + 1) * P],
                                          ones[:], start=True, stop=True)
                mm.then_inc(s_norm_mm, 1)

            def vw_turn(l, b):
                if b == 0:
                    pe.wait_ge(s_w, l * HEADS + HEADS)
                flat = vwT[:, b].rearrange("p h k -> p (h k)")
                for q, quad in enumerate(QUADS):
                    if b >= 1:
                        pe.wait_ge(s_pT, l * (NQ * TILES) + (NQ * (b - 1) + q + 1))
                    for i, (at, n) in enumerate(quad):
                        mm = nc.tensor.transpose(ps[0:n, TURN_BANK + q, i * P:(i + 1) * P], flat[:, at:at + n],
                                                 ident_sb)
                    mm.then_inc(s_vw_mm, 1)

            def scores(l, t):
                b, j = t // TPB, t % TPB
                if t == 0:
                    pe.wait_ge(s_mlo, l * HEADS + HEADS)
                    pe.wait_ge(s_v, l * PAIRS + PAIRS)
                if j == 0:
                    pe.wait_ge(s_xlo, l * BATCH + (b + 1))
                hi, lo = xT_hi[:, b, j * P:(j + 1) * P], xT_lo[:, b, j * P:(j + 1) * P]
                for half in range(2):
                    if t >= 1:
                        pe.wait_ge(s_shift, l * (2 * TILES) + (2 * t + half - 1))
                    for i in range(2):
                        n, h0 = 2 * half + i, HALF * half + HPB * i
                        bank = ps[:, n, 0:HPB * KEYS]
                        cols_hi = m_hi[:, b, h0:h0 + HPB].rearrange("p h k -> p (h k)")
                        cols_lo = m_lo[:, b, h0:h0 + HPB].rearrange("p h k -> p (h k)")
                        nc.tensor.matmul(bank, hi, cols_hi, start=True, stop=False)
                        nc.tensor.matmul(bank, hi, cols_lo, start=False, stop=False)
                        mm = nc.tensor.matmul(bank, lo, cols_hi, start=False, stop=True)
                    mm.then_inc(s_scores, 1)

            def turn(l, t):
                pe.wait_ge(s_prob, l * TILES + (t + 1))
                for q, quad in enumerate(QUADS):
                    n = NQ * t + q
                    if t < BATCH:
                        pe.wait_ge(s_vw, l * (NQ * BATCH) + (n + 1))
                    else:
                        pe.wait_ge(s_pT, l * (NQ * TILES) + (n - 2))
                    for i, (at, rows) in enumerate(quad):
                        mm = nc.tensor.transpose(ps[0:rows, TURN_BANK + q, i * P:(i + 1) * P],
                                                 prob[:, t % RING, at:at + rows], ident_sb)
                    mm.then_inc(s_pT_mm, 1)

            def output(l, part):
                b = part // TPB
                if part % TPB == 0:
                    pe.wait_ge(s_pT, l * (NQ * TILES) + NQ * TPB * (b + 1))
                    if b == 0:
                        pe.wait_ge(s_msum, l + 1)
                    else:
                        pe.wait_ge(s_biased_out, l * BATCH + b)
                for c in range(*OUT_PARTS[part % TPB]):
                    rows = CHUNKS[c][1]
                    mm = nc.tensor.matmul(ps[:, OUT_BANK], vw[0:rows, b, c], pT[0:rows, b % 2, c],
                                          start=(c == 0), stop=(c == len(CHUNKS) - 1))
                if part % TPB == TPB - 1:
                    mm.then_inc(s_out, 1)

            def final(l, b):
                pe.wait_ge(s_resid, LAYERS * BATCH - BATCH + b + 1)
                pe.wait_ge(s_shift, LAYERS * 2 * TILES)
                for j in range(TPB):
                    mm = nc.tensor.transpose(ps[:, b, j * P:(j + 1) * P], xT[:, b, j * P:(j + 1) * P], ident_sb)
                mm.then_inc(s_fin_mm, 1)

            run(pe, {"turn_x": turn_x, "turn_w": turn_w, "kv": kv, "m": m, "w": w, "norm": norm, "vw": vw_turn,
                     "scores": scores, "turn": turn, "output": output, "final": final})

        @block.scalar
        def _(act):
            act.dma_start(idx_sb[:], idx).then_inc(s_idx, 16)
            act.dma_start(ranks_sb, ranks).then_inc(s_idx, 16)
            act.dma_start(ctx_sb[:], ctx.rearrange("b k d -> k b d")).then_inc(s_ctx, 16)
            act.dma_start(vectors_sb[:], vectors).then_inc(s_const, 16)

            def turn_x(_, b):
                act.wait_ge(s_xT_mm, b + 1)
                nc.scalar.copy(xT[:, b], ps[:, 4 + b]).then_inc(s_xT_act, 1)
                act.wait_ge(s_xT_act, b + 1)
                nc.scalar.copy(xT_hi[:, b], xT[:, b]).then_inc(s_xhi, 1)

            def biased_output(l, b):
                act.wait_ge(s_bo, l + 1)
                act.wait_ge(s_out, l * BATCH + (b + 1))
                nc.scalar.activation(xsq[:, b], ps[:, OUT_BANK], ACT.Identity, bias=bo_now[:]).then_inc(s_biased_out, 1)

            def split(l, b):
                act.wait_ge(s_resid, l * BATCH + (b + 1))
                nc.scalar.copy(xT_hi[:, b], xT[:, b]).then_inc(s_xhi, 1)

            def turn_w(l, _):
                act.wait_ge(s_wqT_mm, l * 2 + 1)
                nc.scalar.copy(wqT[:, 0:4].rearrange("p c n -> p (c n)"), ps[:, 0]).then_inc(s_wqT_act, 1)
                act.wait_ge(s_ctx_mm, l * 2 + 1)
                nc.scalar.copy(ctxT[:, 0], ps[:, 2, 0:BK]).then_inc(s_ctx_act, 1)

            def kv(l, c):
                act.wait_ge(s_k_mm, l * PAIRS + (c + 1))
                nc.scalar.copy(kT[:, c], ps[:, 0, 0:BK]).then_inc(s_k, 1)

            def m(l, c):
                for h in (2 * c, 2 * c + 1):
                    act.wait_ge(s_m_mm, l * HEADS + (h + 1))
                    nc.scalar.copy(m_hi[:, :, h], by_batch(ps[:, 2 + h % 2])).then_inc(s_mhi, 1)

            def w(l, c):
                for h in (2 * c, 2 * c + 1):
                    act.wait_ge(s_w_mm, l * HEADS + (h + 1))
                    nc.scalar.copy(vwT[:, :, h], by_batch(ps[:, TURN_BANK + h % 3])).then_inc(s_w, 1)

            def keep_vw(l, b):
                for q in range(NQ):
                    act.wait_ge(s_vw_mm, l * (NQ * BATCH) + (NQ * b + q + 1))
                    copy_quad(nc.scalar.copy, vw[:, b], q, ps[:, TURN_BANK + q]).then_inc(s_vw, 1)

            def exp(l, t):
                if t == 0:
                    act.wait_ge(s_inv, l + 1)
                act.wait_ge(s_shift, l * (2 * TILES) + 2 * (t + 1))
                nc.scalar.activation(prob[:, t % RING], prob[:, t % RING], ACT.Exp, scale=inv[:, t:t + 1]
                                     ).then_inc(s_exp, 1)

            def keep_pT(l, t):
                b, j = t // TPB, t % TPB
                if j == 0 and b >= 2:
                    act.wait_ge(s_out, l * BATCH + (b - 1))
                if t == 0 and not first(l):
                    act.wait_ge(s_out, l * BATCH)
                for q in range(NQ):
                    n = NQ * t + q
                    act.wait_ge(s_pT_mm, l * (NQ * TILES) + (n + 1))
                    copy_quad(nc.scalar.copy, pT[:, b % 2, :, j * P:(j + 1) * P], q, ps[:, TURN_BANK + q]
                              ).then_inc(s_pT, 1)

            def final(l, b):
                if b % 2 == 0:
                    act.wait_ge(s_fin_mm, b + 1)
                    if b:
                        act.wait_ge(s_fin, b)
                    nc.scalar.copy(x_sb[:, TPB * b:TPB * (b + 1)].rearrange("p t c -> p (t c)"), ps[:, b]).then_inc(s_fin, 1)

            run(act, {"turn_x": turn_x, "turn_w": turn_w, "kv": kv, "m": m, "w": w, "vw": keep_vw, "exp": exp,
                      "turn": keep_pT, "residual": biased_output, "split": split, "final": final})

        @block.vector
        def _(dve):
            done = [0]

            def chain(ins):
                done[0] += 1
                ins.then_inc(s_setup, 1)
                dve.wait_ge(s_setup, done[0])

            dve.wait_ge(s_idx, 32)
            chain(nc.vector.tensor_copy(idx_f, idx_sb[:]))
            for w in range(2):
                last = nc.vector.tensor_scalar(hit[:, w], idx_f, key_sb[:, w:w + 1], None, ALU.is_equal)
            chain(last)
            chain(nc.vector.tensor_tensor(hit[:, 0], hit[:, 0], hit[:, 1], ALU.max))
            nc.vector.tensor_tensor(in_b, hit[:, 0, :, 2], hit[:, 0, :, 3], ALU.max)
            chain(nc.vector.tensor_tensor(in_a, hit[:, 0, :, 0], hit[:, 0, :, 1], ALU.max))
            chain(nc.vector.tensor_scalar(not_b, in_b, -1.0, 1.0, ALU.mult, ALU.add))
            chain(nc.vector.tensor_tensor(in_a, in_a, not_b, ALU.mult))
            nc.vector.tensor_tensor(marked, in_a, in_b, ALU.add).then_inc(s_marked, 1)
            dve.wait_ge(s_marked, 1)
            chain(nc.vector.tensor_scalar(plain, marked, -1.0, 1.0, ALU.mult, ALU.add))
            nc.vector.tensor_copy(sides[:, :, 0], in_a.unsqueeze(2).to_broadcast([KEYS, LAYERS, P]))
            nc.vector.tensor_copy(sides[:, :, 1], in_b.unsqueeze(2).to_broadcast([KEYS, LAYERS, P]))
            dve.wait_ge(s_cum_mm, 1)
            nc.vector.tensor_tensor(slot[:, 0], ps[0:KEYS, 4, 0:LAYERS], marked, ALU.mult)
            chain(nc.vector.scalar_tensor_tensor(slot[:, 1], ps[0:KEYS, 4, LAYERS:2 * LAYERS], key_sb[:, 0:1], plain,
                                                 ALU.add, ALU.mult))
            chain(nc.vector.tensor_tensor(slot[:, 2], slot[:, 0], slot[:, 1], ALU.add))
            for l in range(LAYERS):
                last = nc.vector.tensor_scalar(order[:, l], keys_sb, slot[:, 2, l:l + 1], None, ALU.is_equal)
            last.then_inc(s_order, 1)
            dve.wait_ge(s_const, 16)
            nc.vector.tensor_tensor(rowscale[:], small_sb[:, :, NORM_W], small_sb[:, :, SCALE], ALU.mult).then_inc(s_ready, 1)
            chain(nc.vector.tensor_scalar(side_bias[:], mask_sb, 1.0, SUPPRESS, ALU.subtract, ALU.mult))
            dve.wait_ge(s_ind_mm, 1)
            nc.vector.tensor_copy(in_place[:].rearrange("p l s j -> p (l s j)"), ps[:, 5, 0:LAYERS * 2 * MARKED]
                                  ).then_inc(s_ind, 1)
            dve.wait_ge(s_ind, 1)

            def token_bias(l):
                wide = [P, TPB, MARKED]
                for side, to in ((0, bias_a), (1, bias)):
                    last = nc.vector.tensor_tensor(to[:], side_bias[:, side].unsqueeze(2).to_broadcast(wide),
                                                   in_place[:, bass.ds(l, 1), side].to_broadcast(wide), ALU.mult)
                last.then_inc(s_bias, 1)
                dve.wait_ge(s_bias, l * 2 + 1)
                nc.vector.tensor_tensor(bias[:], bias[:], bias_a[:], ALU.add).then_inc(s_bias, 1)

            def scale_wq(l, _):
                dve.wait_ge(s_wq, (l + 1) * 16)
                if first(l):
                    dve.wait_ge(s_ready, 1)
                nc.vector.tensor_scalar(wq_sb[:], wq_sb[:], rowscale[:, bass.ds(l, 1)], None, ALU.mult).then_inc(s_wqs, 1)
                token_bias(l)


            def turn_w(l, _):
                dve.wait_ge(s_wqT_mm, l * 2 + 2)
                nc.vector.tensor_copy(wqT[:, 4:8].rearrange("p c n -> p (c n)"), ps[:, 1]).then_inc(s_wqT_dve, 1)
                dve.wait_ge(s_ctx_mm, l * 2 + 2)
                nc.vector.tensor_copy(ctxT[:, 1], ps[:, 3, 0:BK]).then_inc(s_ctx_dve, 1)

            def kv(l, c):
                dve.wait_ge(s_v_mm, l * PAIRS + (c + 1))
                nc.vector.tensor_copy(vT[:, c], ps[:, 1, 0:BK]).then_inc(s_v, 1)

            def m(l, c):
                for h in (2 * c, 2 * c + 1):
                    dve.wait_ge(s_mhi, l * HEADS + (h + 1))
                    nc.vector.tensor_tensor(m_lo[:, :, h], by_batch(ps[:, 2 + h % 2]), m_hi[:, :, h].bitcast(F32),
                                            ALU.subtract).then_inc(s_mlo, 1)

            def norm(l, _):
                dve.wait_ge(s_norm_mm, l + 1)
                nc.vector.tensor_scalar(msum[:], ps[:, OUT_BANK, 0:TILES], small_sb[:, bass.ds(l, 1), MEAN],
                                        small_sb[:, bass.ds(l, 1), EPS], ALU.mult, ALU.add).then_inc(s_msum, 1)
                nc.vector.tensor_copy(bo_now[:], small_sb[:, bass.ds(l, 1), BO]).then_inc(s_bo, 1)

            def add_bias(l, t):
                if t == 0:
                    dve.wait_ge(s_bias, l * 2 + 2)
                for half in range(2):
                    dve.wait_ge(s_scores, l * (2 * TILES) + (2 * t + half + 1))
                    places = half_banks(half)[:, :, :, 0:MARKED]
                    nc.vector.tensor_tensor(places, places, bias[:, t % TPB].unsqueeze(1).unsqueeze(1).to_broadcast(
                        [P, 2, HPB, MARKED]), ALU.add).then_inc(s_biased, 1)

            def shift(l, t):
                at = l * (2 * TILES) + 2 * t
                own_max = [mx[:, t % RING, HALF * half:HALF * (half + 1)].rearrange("p (a h) -> p a h", a=2)
                           for half in range(2)]
                for half in range(2):
                    dve.wait_ge(s_biased, at + (half + 1))
                    nc.vector.tensor_reduce(own_max[half], half_banks(half), AX.X, ALU.max).then_inc(s_max, 1)
                if t >= RING:
                    dve.wait_ge(s_pT_mm, l * (NQ * TILES) + NQ * (t - RING + 1))
                for half in range(2):
                    dve.wait_ge(s_max, at + (half + 1))
                    to = prob[:, t % RING, HALF * KEYS * half:HALF * KEYS * (half + 1)]
                    nc.vector.tensor_tensor(to.rearrange("p (a h k) -> p a h k", a=2, k=KEYS), half_banks(half),
                                            own_max[half].unsqueeze(3).to_broadcast([P, 2, HPB, KEYS]),
                                            ALU.subtract).then_inc(s_shift, 1)

            def denominators(l, t):
                dve.wait_ge(s_exp, l * TILES + (t + 1))
                nc.vector.tensor_reduce(tot[:, t % RING], by_head(prob[:, t % RING]), AX.X, ALU.add).then_inc(s_sum, 1)

            def reciprocals(l, t):
                dve.wait_ge(s_sum, l * TILES + (t + 1))
                nc.vector.reciprocal(rec[:, t % RING], tot[:, t % RING]).then_inc(s_rec, 1)

            def final(l, b):
                if b % 2:
                    dve.wait_ge(s_fin_mm, b + 1)
                    dve.wait_ge(s_fin, b)
                    nc.vector.tensor_copy(x_sb[:, TPB * b:TPB * (b + 1)].rearrange("p t c -> p (t c)"), ps[:, b]
                                          ).then_inc(s_fin, 1)

            run(dve, {"scale": scale_wq, "turn_w": turn_w, "kv": kv, "m": m, "norm": norm, "scores": add_bias,
                      "shift": shift, "exp": denominators, "normalise": reciprocals, "final": final})

        @block.gpsimd
        def _(pool):
            nc.gpsimd.memset(ones[:], 1.0)
            nc.gpsimd.memset(halfs[:], -0.5).then_inc(s_half, 1)
            pool.wait_ge(s_half, 1)

            def turn_x(_, b):
                pool.wait_ge(s_xhi, b + 1)
                nc.gpsimd.tensor_tensor(xT_lo[:, b], xT[:, b], xT_hi[:, b].bitcast(F32), ALU.subtract).then_inc(s_xlo, 1)
                nc.gpsimd.tensor_tensor(xsq[:, b], xT[:, b], xT[:, b], ALU.mult).then_inc(s_xsq, 1)

            def residual(l, b):
                pool.wait_ge(s_biased_out, l * BATCH + (b + 1))
                nc.gpsimd.tensor_tensor(xT[:, b], xT[:, b], xsq[:, b], ALU.add).then_inc(s_resid, 1)

            def split(l, b):
                pool.wait_ge(s_resid, l * BATCH + (b + 1))
                nc.gpsimd.tensor_tensor(xsq[:, b], xT[:, b], xT[:, b], ALU.mult).then_inc(s_xsq, 1)
                pool.wait_ge(s_xhi, (l + 1) * BATCH + (b + 1))
                nc.gpsimd.tensor_tensor(xT_lo[:, b], xT[:, b], xT_hi[:, b].bitcast(F32), ALU.subtract).then_inc(s_xlo, 1)

            def norm(l, _):
                pool.wait_ge(s_msum, l + 1)
                nc.gpsimd.tensor_tensor(inv[:], msum[:], halfs[:], ALU.pow).then_inc(s_inv, 1)

            def normalise(l, t):
                pool.wait_ge(s_rec, l * TILES + (t + 1))
                nc.gpsimd.tensor_tensor(by_head(prob[:, t % RING]), by_head(prob[:, t % RING]),
                                        rec[:, t % RING].unsqueeze(2).to_broadcast([P, HEADS, KEYS]),
                                        ALU.mult).then_inc(s_prob, 1)

            run(pool, {"turn_x": turn_x, "normalise": normalise, "residual": residual, "split": split, "norm": norm})


def copy_quad(copy, dst, q, bank):
    full = [c for c in range(4 * q, min(4 * q + 4, len(CHUNKS))) if CHUNKS[c][1] == P]
    last = copy(dst[:, full[0]:full[-1] + 1], bank[:, 0:len(full) * P].rearrange("p (c n) -> p c n", n=P))
    for c in range(4 * q + len(full), min(4 * q + 4, len(CHUNKS))):
        rows, at = CHUNKS[c][1], (c - 4 * q) * P
        last = copy(dst[0:rows, c], bank[0:rows, at:at + P])
    return last


def lay_out(inputs):
    import numpy as np

    def heads64(w, axis):
        shape = list(w.shape)
        shape[axis:axis + 1] = [HEADS, HDIM]
        full = np.zeros(shape, w.dtype)
        small = list(w.shape)
        small[axis:axis + 1] = [HEADS, w.shape[axis] // HEADS]
        at = [slice(None)] * len(shape)
        at[axis + 1] = slice(0, w.shape[axis] // HEADS)
        full[tuple(at)] = w.reshape(small)
        shape = list(w.shape)
        shape[axis] = INNER
        return full.reshape(shape)

    def repeated(w):
        kv = 4
        d = w.shape[1] // kv
        return np.repeat(w.reshape(w.shape[0], kv, d), HEADS // kv, axis=1).reshape(w.shape[0], HEADS * d)

    big = ("L0_xattn_", "L2_xattn_", "L3_xattn_")
    a = {k: np.asarray(v) for k, v in inputs.items()}

    def stack(name, one):
        return np.stack([a[big[0] + name], one, a[big[1] + name], a[big[2] + name]])

    d = {"x": a["x"], "ctx": a["ctx_2048"]}
    d["wq"] = stack("Wq", heads64(a["L1_xattn_wq"], 1))
    d["wk"] = stack("Wk", heads64(repeated(a["L1_xattn_wk"]), 1))
    d["wv"] = stack("Wv", heads64(repeated(a["L1_xattn_wv"]), 1))
    d["wo"] = stack("Wo", heads64(a["L1_xattn_wo"], 0))
    zeros, ones = np.zeros((C,), np.float32), np.ones((C,), np.float32)
    plain, normed = (HDIM ** -0.5, 0.0, 1.0), (8 ** -0.5, 1.0 / C, 1e-5)
    small = np.zeros((P, LAYERS, 5), np.float32)
    small[:, :, NORM_W] = np.stack([ones, a["L1_xattn_norm_w"], ones, ones], axis=1)
    small[:, :, SCALE:EPS + 1] = np.array([plain, normed, plain, plain], np.float32)
    small[:, :, BO] = stack("bo", zeros).T
    none = np.full((2,), -1000, np.int32)
    rows = [np.concatenate([a[name + "token_indices_A"], a[name + "token_indices_B"]] if name else [none, none])
            for name in ("L0_xattn_", None, "L2_xattn_", "L3_xattn_")]
    d["idx"] = np.broadcast_to(np.stack(rows), (KEYS, LAYERS, 4))
    masks = np.stack([a["mask_S_fk1"], a["mask_S_fk0"]]).reshape(2, TPB, P).transpose(2, 0, 1)
    d["vectors"] = np.concatenate([np.eye(P, dtype=np.float32), small.reshape(P, -1), masks.reshape(P, -1)], axis=1)
    at = np.arange(KEYS, dtype=np.float32)
    d["ranks"] = np.concatenate([np.stack([at, at - KEYS], axis=1), np.broadcast_to(at, (KEYS, KEYS)),
                                 (at[:, None] < at[None, :]), (at[:, None] >= at[None, :])], axis=1).astype(np.float32)
    return d


def kernel(**inputs):
    import numpy as np
    import concourse.bacc as bacc
    from concourse.bass_utils import run_bass_kernel_spmd

    nc = bacc.Bacc("TRN2", target_bir_lowering=False, num_devices=1)
    arrays, aps = {}, {}
    for name, value in lay_out(inputs).items():
        value = np.ascontiguousarray(value)
        arrays[f"in_{name}"] = value
        aps[name] = nc.dram_tensor(f"in_{name}", value.shape, mybir.dt.from_np(value.dtype), kind="ExternalInput").ap()
    out = nc.dram_tensor("out_x", (BATCH, SEQ, C), F32, kind="ExternalOutput").ap()
    build(nc, out=out, **aps)
    result = run_bass_kernel_spmd(nc, [arrays], core_ids=[0])
    return result.results[0]["out_x"]
```

```python
from contextlib import ExitStack

import concourse.bass as bass
from concourse import mybir

F32 = mybir.dt.float32
F32R = mybir.dt.float32r
I32 = mybir.dt.int32
ALU = mybir.AluOpType
ACT = mybir.ActivationFunctionType
AX = mybir.AxisListType

LAYERS = 4
BATCH, SEQ, C = 4, 512, 128
KEYS, CTX = 77, 256
HEADS, HDIM = 16, 64
INNER = HEADS * HDIM
P = 128
TILES = BATCH * SEQ // P
TPB = SEQ // P
HK = HEADS * KEYS
BK = BATCH * KEYS
CHUNKS = [(c * P, min(P, HK - c * P)) for c in range((HK + P - 1) // P)]
QUADS = [CHUNKS[0:4], CHUNKS[4:8], CHUNKS[8:10]]
NQ = len(QUADS)
HPB = 4
HALF = 2 * HPB
OUT_PARTS = [(0, 3), (3, 5), (5, 8), (8, 10)]
KC = CTX // P
PAIRS = INNER // P
SUPPRESS = 20.0
NORMED, NORM_EPS = 1, 1e-5
RING = 4
MARKED = 4
NORM_W, SCALE, BO = range(3)

TURN_BANK, OUT_BANK, SUMS_BANK = 4, 7, 6
M_BANK, M_BANKS, V_BANK, X_BANK = 2, 4, 7, 6
SUMS_BEFORE = {0: 10, 1: 15}


def now(*steps):
    return [(step, n, 0) for step, n in steps]


def ahead(*steps):
    return [(step, n, 1) for step, n in steps]


def tile_step(s, *beside):
    steps = [("scores", s + 3)] if s + 3 < TILES else []
    steps += [("normalise", s + 1)] if 0 <= s + 1 < TILES else []
    steps += [("shift", s + 3)] if s + 3 < TILES else []
    exp = [("exp", s + 2)] if 0 <= s + 2 < TILES else []
    early = s == 13
    steps += exp if not early else []
    steps += [("residual", s // TPB - 2)] if s >= 8 and s % TPB == 0 else []
    steps += list(beside)
    turn, output = [("turn", s)] if s >= 0 else [], [("output", s - TPB)] if s >= TPB else []
    steps += turn + exp + output if early else output + turn if s >= TILES - 2 else turn + output
    steps += [("split", s // TPB - 2)] if s >= 8 and s % TPB == 1 else []
    return steps


BESIDE = {-3: [("w", 0), ("v", 3), ("w", 1)], -2: [("v", 4), ("w", 2), ("v", 5)], -1: [("w", 3), ("v", 6), ("w", 4)],
          0: [("v", 7), ("w", 5)], 1: [("w", 6), ("w", 7)], 2: [("vw", 0)], 3: [("vw", 1)], 4: [("vw", 2)],
          5: [("vw", 3)]}
W_BEFORE = {0: 5, 1: 7}
W_AFTER = {6: 0}
VW_TILE = 2


def rest(more={}):
    return ahead(("norm", 0), *[x for s in (-3, -2, -1) for x in tile_step(s, *BESIDE[s], *more.get(s, []))])


FIRST = ahead(("scale", 0), ("split_w", 0), ("turn_ctx", 0), ("split_q", 0), ("k", 0), ("k", 1),
              ("marks", 0), ("bias", 0), ("split_w", 1), ("m", 0), ("k", 2), ("m", 1), ("k", 3), ("m", 2), ("turn_x", 0),
              ("k", 4), ("m", 3), ("k", 5), ("split_w", 2), ("m", 4), ("turn_x", 1), ("k", 6), ("m", 5), ("v", 0), ("k", 7),
              ("m", 6), ("v", 1), ("m", 7), ("split_w", 3), ("v", 2)) + rest({-3: [("turn_x", 2)], -2: [("turn_x", 3)]})


def layer(sums_of_squares):
    split_at = {6: 0, 7: 1, 10: 2, 11: 3}
    row_before = {tile: row for row, tile in SUMS_BEFORE.items()} if sums_of_squares else {}
    steps = []
    for s in range(13):
        steps += now(*tile_step(s, *BESIDE.get(s, []))) + (ahead(("split_w", split_at[s])) if s in split_at else [])
    steps += ahead(("scale", 0), ("bias", 0)) + now(*tile_step(13)) + ahead(("turn_ctx", 0)) + now(*tile_step(14))
    steps += ahead(("split_q", 0), ("k", 0)) + now(*tile_step(15)) + ahead(("k", 1)) + now(("residual", 2))
    steps += ahead(("m", 0), ("k", 2)) + now(("output", 12)) + ahead(("m", 1), ("k", 3)) + now(("split", 2), ("output", 13))
    steps += ahead(("m", 2), ("k", 4)) + now(("output", 14)) + ahead(*[("sums", 2)] * sums_of_squares, ("m", 3), ("k", 5))
    steps += now(("output", 15)) + ahead(("m", 4), ("k", 6)) + now(("residual", 3)) + ahead(("m", 5), ("k", 7), ("v", 0))
    steps += now(("split", 3)) + ahead(("m", 6), ("v", 1), ("m", 7), ("v", 2), *[("sums", 3)] * sums_of_squares) + rest()
    return [x for step in steps
            for x in (ahead(("sums", row_before[step[1]])) if step[0] == "turn" and step[1] in row_before else []) + [step]]


LAYER_BEFORE_NORMED, LAYER = layer(True), layer(False)
LAST = now(
    *[x for s in range(TILES) for x in tile_step(s, *BESIDE.get(s, [])) if x[0] != "split"],
    ("residual", 2), ("final", 0), ("final", 1), ("output", 12), ("output", 13), ("final", 2), ("output", 14),
    ("output", 15), ("residual", 3), ("final", 3))


def build(nc, x, ctx, wq, wk, wv, wo, vectors, idx, ranks, out):
    with ExitStack() as stack:
        def sb(name, shape, dt=F32):
            return stack.enter_context(nc.sbuf_tensor(name, shape, dt))

        def lent(name, shape, dt=F32):
            with nc.sbuf_tensor(name, shape, dt) as tensor:
                return tensor

        def sem(name):
            return stack.enter_context(nc.semaphore(name))

        ps = stack.enter_context(nc.psum_tensor("ps", [P, 8, 512], F32))

        vectors_sb = sb("vectors_sb", [P, P + 3 * LAYERS + 2 * TPB])
        ident_sb = vectors_sb[:, 0:P]
        small_sb = vectors_sb[:, P:P + 3 * LAYERS].rearrange("p (l n) -> p l n", n=3)
        mask_sb = vectors_sb[:, P + 3 * LAYERS:].rearrange("p (s j) -> p s j", j=TPB)
        xsq = sb("xsq", [P, SEQ])
        xT = sb("xT", [P, BATCH, SEQ])
        xT_hi = sb("xT_hi", [P, BATCH, SEQ], F32R)
        xT_lo = sb("xT_lo", [P, BATCH, SEQ], F32R)
        ones = sb("ones", [P, 1])
        halfs = sb("halfs", [P, TILES])
        sumsq = sb("sumsq", [P, TILES])
        msum = sb("msum", [P, TILES])
        inv = sb("inv", [P, TILES])
        scale_now = sb("scale_now", [P, 1])
        bo_now = sb("bo_now", [P, 1])
        ctx_sb = sb("ctx_sb", [KEYS, BATCH, CTX])
        ctx_hi = sb("ctx_hi", [P, KC, BK], F32R)
        ctx_lo = sb("ctx_lo", [P, KC, BK], F32R)
        wq_sb = lent("wq_sb", [P, PAIRS, C])
        wq_lo = sb("wq_lo", [P, PAIRS, C], F32R)
        wk_sb = lent("wk_sb", [P, KC, INNER])
        wk_lo = sb("wk_lo", [P, KC, INNER], F32R)
        wv_sb = lent("wv_sb", [P, KC, INNER])
        wv_lo = sb("wv_lo", [P, KC, INNER], F32R)
        wv_hi = sb("wv_hi", [P, KC, INNER], F32R)
        wo_sb = sb("wo_sb", [P, PAIRS, C])
        m_hi = sb("m_hi", [P, BATCH, HEADS, KEYS], F32R)
        m_lo = sb("m_lo", [P, BATCH, HEADS, KEYS], F32R)
        vwT = lent("vwT", [P, BATCH, HEADS, KEYS])
        kT_hi = sb("kT_hi", [P, PAIRS, BK], F32R)
        wk_hi = sb("wk_hi", [P, KC, INNER], F32R)
        sb("vwT_end", [P, 2 * HK - KC * INNER])
        vw = sb("vw", [P, BATCH, len(CHUNKS), C])
        vT = vw[:, 0:2].rearrange("p b c n -> p (b c n)")[:, 0:PAIRS * BK].rearrange("p (c n) -> p c n", n=BK)
        prob = lent("prob", [P, RING, HK])
        kT_lo = sb("kT_lo", [P, PAIRS, BK], F32R)
        wq_hi = sb("wq_hi", [P, PAIRS, C], F32R)
        sb("prob_end", [P, 2 * HK - PAIRS * C])
        mx = sb("mx", [P, RING, HEADS])
        tot = sb("tot", [P, RING, HEADS])
        rec = sb("rec", [P, RING, HEADS])
        pT = sb("pT", [P, 2, len(CHUNKS), SEQ])
        x_sb = pT[:, 0].rearrange("p c n -> p (c n)")[:, 0:TILES * C].rearrange("p (t c) -> p t c", c=C)
        used = [0]

        def scratch(*shape):
            size = 1
            for n in shape:
                size *= n
            at = used[0]
            used[0] += size
            flat = pT[0:KEYS, 1].rearrange("p c n -> p (c n)")[:, at:at + size]
            if len(shape) == 1:
                return flat
            names = "abc"[:len(shape)]
            return flat.rearrange(f"p ({' '.join(names)}) -> p {' '.join(names)}", **dict(zip(names, shape)))

        side_bias = sb("side_bias", [P, 2, TPB])
        in_place = sb("in_place", [P, LAYERS, 2, MARKED])
        bias_a = sb("bias_a", [P, TPB, MARKED])
        bias = sb("bias", [P, TPB, MARKED])
        ranks_sb = scratch(2 + 3 * KEYS)
        key_sb = ranks_sb[:, 0:2]
        keys_sb = ranks_sb[:, 2:2 + KEYS]
        before_sb = ranks_sb[:, 2 + KEYS:2 + 2 * KEYS]
        upto_sb = ranks_sb[:, 2 + 2 * KEYS:]
        idx_sb = sb("idx_sb", [KEYS, LAYERS, 4], I32)
        idx_f = scratch(LAYERS, 4)
        hit = scratch(2, LAYERS, 4)
        in_b = scratch(LAYERS)
        not_b = scratch(LAYERS)
        in_a = scratch(LAYERS)
        marked = scratch(LAYERS)
        plain = scratch(LAYERS)
        slot = scratch(3, LAYERS)
        sides = scratch(LAYERS, 2, MARKED)
        key_ones = scratch(P)
        order = sb("order", [KEYS, LAYERS, KEYS])

        s_idx = sem("s_idx")
        s_const = sem("s_const")
        s_ctx = sem("s_ctx")
        s_x = sem("s_x")
        s_wq, s_wk, s_wv, s_wo = sem("s_wq"), sem("s_wk"), sem("s_wv"), sem("s_wo")
        s_stored = sem("s_stored")
        s_zero = sem("s_zero")
        s_half = sem("s_half")
        s_setup = sem("s_setup")
        s_marked = sem("s_marked")
        s_cum_mm = sem("s_cum_mm")
        s_order = sem("s_order")
        s_sides = sem("s_sides")
        s_ind_mm = sem("s_ind_mm")
        s_ind = sem("s_ind")
        s_bias = sem("s_bias")
        s_biased = sem("s_biased")
        s_xT_mm, s_xT_act = sem("s_xT_mm"), sem("s_xT_act")
        s_xhi, s_xlo = sem("s_xhi"), sem("s_xlo")
        s_xsq = sem("s_xsq")
        s_norm_mm, s_sums = sem("s_norm_mm"), sem("s_sums")
        s_msum, s_inv = sem("s_msum"), sem("s_inv")
        s_scale = sem("s_scale")
        s_qhi, s_qlo = sem("s_qhi"), sem("s_qlo")
        s_whi, s_wlo = sem("s_whi"), sem("s_wlo")
        s_ctx_mm = sem("s_ctx_mm")
        s_ctx_hi, s_ctx_lo = sem("s_ctx_hi"), sem("s_ctx_lo")
        s_k_mm, s_khi, s_klo = sem("s_k_mm"), sem("s_khi"), sem("s_klo")
        s_v_mm, s_v = sem("s_v_mm"), sem("s_v")
        s_m_mm, s_mhi, s_mlo = sem("s_m_mm"), sem("s_mhi"), sem("s_mlo")
        s_w_mm, s_w = sem("s_w_mm"), sem("s_w")
        s_vw_mm, s_vw = sem("s_vw_mm"), sem("s_vw")
        s_scores = sem("s_scores")
        s_max = sem("s_max")
        s_shift = sem("s_shift")
        s_exp, s_sum = sem("s_exp"), sem("s_sum")
        s_rec, s_prob = sem("s_rec"), sem("s_prob")
        s_pT_mm, s_pT = sem("s_pT_mm"), sem("s_pT")
        s_out = sem("s_out")
        s_bo = sem("s_bo")
        s_biased_out = sem("s_biased_out")
        s_resid = sem("s_resid")
        s_fin_mm = sem("s_fin_mm")
        s_fin_act, s_fin_dve = sem("s_fin_act"), sem("s_fin_dve")

        x_dram = x.rearrange("b (t p) c -> p (b t) c", p=P)
        out_dram = out.rearrange("b (t p) c -> p (b t) c", p=P)

        block = stack.enter_context(nc.Block())

        def by_head(ap):
            return ap.rearrange("p (h k) -> p h k", k=KEYS)

        def by_batch(bank):
            return bank[:, 0:BK].rearrange("p (b k) -> p b k", k=KEYS)

        def half_banks(h):
            return ps[:, 2 * h:2 * h + 2, 0:HPB * KEYS].rearrange("p a (h k) -> p a h k", k=KEYS)

        def tiles_of(tiles, b, half):
            return tiles[:, TPB * b + 2 * half:TPB * b + 2 * half + 2]

        def out_rows(b, half):
            return tiles_of(x_sb, b, half)

        def columns(w, i):
            return w[i // 2][:, :, i % 2 * (INNER // 2):(i % 2 + 1) * (INNER // 2)]

        def walk(schedule, l, does):
            for step, n, later in schedule:
                if step in does:
                    does[step](l + later, n)

        def run(engine, does):
            walk(FIRST, -1, does)
            walk(LAYER_BEFORE_NORMED, 0, does)
            with engine.Fori(1, LAYERS - 1) as l:
                walk(LAYER, l, does)
            walk(LAST, LAYERS - 1, does)

        def first(l):
            return isinstance(l, int) and l == 0

        def is_last(l):
            return isinstance(l, int) and l == LAYERS - 1

        def normed(l):
            return isinstance(l, int) and l == NORMED

        def pairs_each(l):
            return 2 if normed(l) else 1

        def has_k(l, n):
            return l * PAIRS + pairs_each(l) * (n + 1)

        def skips_k(l, n):
            return n >= PAIRS // pairs_each(l)

        @block.sync
        def _(sp):
            sp.dma_start(idx_sb[:], idx).then_inc(s_idx, 16)
            sp.dma_start(vectors_sb[:], vectors).then_inc(s_const, 16)
            for l in range(LAYERS):
                if l >= 1:
                    sp.wait_ge(s_w_mm, l * HEADS)
                sp.dma_start(wk_sb[:], wk[l].rearrange("(k p) n -> p k n", p=P)).then_inc(s_wk, 16)
                sp.dma_start(wq_sb[:], wq[l].rearrange("(c p) n -> p c n", p=P)).then_inc(s_wq, 16)
                if l == 0:
                    sp.dma_start(x_sb, x_dram).then_inc(s_x, 16)
                sp.dma_start(wv_sb[:], wv[l].rearrange("(k p) n -> p k n", p=P)).then_inc(s_wv, 16)
                sp.dma_start(wo_sb[:], wo[l].rearrange("(c p) n -> p c n", p=P)).then_inc(s_wo, 16)
            for b in range(BATCH):
                for half, s_fin in enumerate((s_fin_act, s_fin_dve)):
                    sp.wait_ge(s_fin, b + 1)
                    sp.dma_start(tiles_of(out_dram, b, half), out_rows(b, half)).then_inc(s_stored, 16)
            sp.wait_ge(s_stored, 16 * BATCH * 2)

        @block.tensor
        def _(pe):
            def keep_warm(n):
                for _ in range(n):
                    nc.tensor.matmul(ps[:, V_BANK], xT[:, 0, 0:P], xT[:, 0], start=True, stop=True)

            pe.wait_ge(s_zero, 1)
            keep_warm(2)
            pe.wait_ge(s_idx, 32)
            pe.wait_ge(s_marked, 1)
            nc.tensor.matmul(ps[0:KEYS, 4, 0:LAYERS], before_sb, marked, start=True, stop=True)
            nc.tensor.matmul(ps[0:KEYS, 4, LAYERS:2 * LAYERS], upto_sb, marked,
                             start=True, stop=True).then_inc(s_cum_mm, 1)

            def marks(_, n):
                pe.wait_ge(s_sides, 1)
                pe.wait_ge(s_half, 1)
                nc.tensor.matmul(ps[:, X_BANK, 0:LAYERS * 2 * MARKED], key_ones, sides.rearrange("p l s j -> p (l s j)"),
                                 start=True, stop=True).then_inc(s_ind_mm, 1)

            def turn_ctx(l, _):
                if first(l):
                    keep_warm(2)
                    pe.wait_ge(s_order, 1)
                    pe.wait_ge(s_ctx, 16)
                else:
                    pe.wait_ge(s_shift, l * (2 * TILES))
                for kc in range(KC):
                    for b in range(BATCH):
                        mm = nc.tensor.matmul(ps[:, 2 + kc, b * KEYS:(b + 1) * KEYS], ctx_sb[:, b, kc * P:(kc + 1) * P],
                                              order[:, l], start=True, stop=True)
                    mm.then_inc(s_ctx_mm, 1)

            def turn_x(_, b):
                if b == 0:
                    pe.wait_ge(s_x, 16)
                    pe.wait_ge(s_const, 16)
                    pe.wait_ge(s_ind, 1)
                else:
                    pe.wait_ge(s_xT_act, b)
                for j in range(TPB):
                    mm = nc.tensor.transpose(ps[:, X_BANK, j * P:(j + 1) * P], x_sb[:, TPB * b + j], ident_sb)
                mm.then_inc(s_xT_mm, 1)

            def context_product(bank, c, hi, lo, second_ready=None):
                passes = [(w[:, kc, c * P:(c + 1) * P], context[:, kc])
                          for kc in range(KC) for w, context in ((hi, ctx_hi), (hi, ctx_lo), (lo, ctx_hi))]
                for n, (w, context) in enumerate(passes):
                    if second_ready is not None and n == len(passes) // KC:
                        pe.wait_ge(s_ctx_lo, second_ready)
                    mm = nc.tensor.matmul(bank, w, context, start=(n == 0), stop=(n == len(passes) - 1))
                return mm

            def k(l, c):
                if skips_k(l, c):
                    return
                if c % 4 == 0:
                    pe.wait_ge(s_wlo, l * 4 + (c // 4 + 1))
                if c == 0:
                    pe.wait_ge(s_ctx_lo, l * KC + 1)
                if c >= 2:
                    pe.wait_ge(s_klo, has_k(l, c - 2))
                context_product(ps[:, c % 2, 0:BK], c, wk_hi, wk_lo, l * KC + KC if c == 0 else None
                                ).then_inc(s_k_mm, pairs_each(l))

            def v(l, c):
                if c % 4 == 0:
                    pe.wait_ge(s_wlo, l * 4 + (c // 4 + 3))
                if c >= 1:
                    pe.wait_ge(s_v, l * PAIRS + c)
                elif not first(l):
                    pe.wait_ge(s_biased_out, l * BATCH)
                context_product(ps[:, V_BANK, 0:BK], c, wv_hi, wv_lo).then_inc(s_v_mm, 1)

            def m(l, c):
                n = c // pairs_each(l)
                pe.wait_ge(s_klo, has_k(l, n))
                if c == 0:
                    pe.wait_ge(s_qlo, l + 1)
                for h in (2 * c, 2 * c + 1):
                    rows = slice(HDIM * (h % 2), HDIM * (h % 2) + HDIM)
                    if h >= M_BANKS:
                        pe.wait_ge(s_mlo, l * HEADS + (h - M_BANKS + 1))
                    if h == 2 and not first(l):
                        pe.wait_ge(s_pT, l * (NQ * TILES))
                    bank = ps[:, M_BANK + h % M_BANKS, 0:BK]
                    nc.tensor.matmul(bank, wq_hi[rows, c], kT_hi[rows, n], start=True, stop=False)
                    nc.tensor.matmul(bank, wq_hi[rows, c], kT_lo[rows, n], start=False, stop=False)
                    nc.tensor.matmul(bank, wq_lo[rows, c], kT_hi[rows, n], start=False, stop=True).then_inc(s_m_mm, 1)

            def w(l, c):
                if c == 0:
                    pe.wait_ge(s_wo, (l + 1) * 16)
                    pe.wait_ge(s_mlo, l * HEADS + HEADS)
                pe.wait_ge(s_v, l * PAIRS + (c + 1))
                for i in range(2):
                    r, h = HDIM * i, 2 * c + i
                    if h >= 2:
                        pe.wait_ge(s_w, l * HEADS + (h - 1))
                    if c in W_AFTER:
                        pe.wait_ge(s_pT, l * (NQ * TILES) + (NQ * W_AFTER[c] + i + 1))
                    nc.tensor.matmul(ps[:, TURN_BANK + i, 0:BK], wo_sb[r:r + HDIM, c], vT[r:r + HDIM, c],
                                     start=True, stop=True).then_inc(s_w_mm, 1)

            def sums(l, b):
                pe.wait_ge(s_xsq, b + 1)
                if b == 3:
                    pe.wait_ge(s_sums, b)
                else:
                    pe.wait_ge(s_pT, (l - 1) * (NQ * TILES) + NQ * SUMS_BEFORE.get(b, TILES))
                for j in range(TPB):
                    mm = nc.tensor.matmul(ps[:, SUMS_BANK, j:j + 1], xsq[:, j * P:(j + 1) * P], ones[:],
                                          start=True, stop=True)
                mm.then_inc(s_norm_mm, 1)

            def vw_turn(l, b):
                if b == 0:
                    pe.wait_ge(s_w, l * HEADS + HEADS)
                flat = vwT[:, b].rearrange("p h k -> p (h k)")
                for q, quad in enumerate(QUADS):
                    pe.wait_ge(s_pT, l * (NQ * TILES) + (NQ * (VW_TILE + b - 1) + q + 1))
                    for i, (at, n) in enumerate(quad):
                        mm = nc.tensor.transpose(ps[0:n, TURN_BANK + q, i * P:(i + 1) * P], flat[:, at:at + n],
                                                 ident_sb)
                    mm.then_inc(s_vw_mm, 1)

            def scores(l, t):
                b, j = t // TPB, t % TPB
                if t == 0:
                    pe.wait_ge(s_klo, l * PAIRS + PAIRS)
                    pe.wait_ge(s_mlo, l * HEADS + HALF)
                if j == 0:
                    pe.wait_ge(s_xlo, l * BATCH + (b + 1))
                hi, lo = xT_hi[:, b, j * P:(j + 1) * P], xT_lo[:, b, j * P:(j + 1) * P]
                for half in range(2):
                    if t == 0 and half == 1:
                        pe.wait_ge(s_mlo, l * HEADS + HEADS)
                    if t >= 1:
                        pe.wait_ge(s_shift, l * (2 * TILES) + (2 * t + half - 1))
                    for i in range(2):
                        n, h0 = 2 * half + i, HALF * half + HPB * i
                        bank = ps[:, n, 0:HPB * KEYS]
                        cols_hi = m_hi[:, b, h0:h0 + HPB].rearrange("p h k -> p (h k)")
                        cols_lo = m_lo[:, b, h0:h0 + HPB].rearrange("p h k -> p (h k)")
                        nc.tensor.matmul(bank, hi, cols_hi, start=True, stop=False)
                        nc.tensor.matmul(bank, hi, cols_lo, start=False, stop=False)
                        mm = nc.tensor.matmul(bank, lo, cols_hi, start=False, stop=True)
                    mm.then_inc(s_scores, 1)

            def turn(l, t):
                pe.wait_ge(s_prob, l * TILES + (t + 1))
                for q, quad in enumerate(QUADS):
                    n = NQ * t + q
                    if t in W_BEFORE and q < 2:
                        pe.wait_ge(s_w, l * HEADS + (2 * W_BEFORE[t] + q + 1))
                    elif t == 0:
                        pe.wait_ge(s_exp, l * TILES + 2)
                    elif VW_TILE <= t < VW_TILE + BATCH:
                        pe.wait_ge(s_vw, l * (NQ * BATCH) + (n + 1 - NQ * VW_TILE))
                    else:
                        pe.wait_ge(s_pT, l * (NQ * TILES) + (n - 2))
                    for row, before in SUMS_BEFORE.items():
                        if t == before and TURN_BANK + q == SUMS_BANK and first(l):
                            pe.wait_ge(s_sums, row + 1)
                    for i, (at, rows) in enumerate(quad):
                        mm = nc.tensor.transpose(ps[0:rows, TURN_BANK + q, i * P:(i + 1) * P],
                                                 prob[:, t % RING, at:at + rows], ident_sb)
                    mm.then_inc(s_pT_mm, 1)

            def output(l, part):
                b = part // TPB
                """A part of the chunks of the output product of a batch row."""
                if part % TPB == 0:
                    pe.wait_ge(s_pT, l * (NQ * TILES) + NQ * TPB * (b + 1))
                    if b == 0:
                        pe.wait_ge(s_v, l * PAIRS + PAIRS)
                    else:
                        pe.wait_ge(s_biased_out, l * BATCH + b)
                for c in range(*OUT_PARTS[part % TPB]):
                    rows = CHUNKS[c][1]
                    mm = nc.tensor.matmul(ps[:, OUT_BANK], vw[0:rows, b, c], pT[0:rows, b % 2, c],
                                          start=(c == 0), stop=(c == len(CHUNKS) - 1))
                if part % TPB == TPB - 1:
                    mm.then_inc(s_out, 1)

            def final(l, b):
                pe.wait_ge(s_resid, LAYERS * BATCH - BATCH + b + 1)
                if b == 0:
                    pe.wait_ge(s_shift, LAYERS * 2 * TILES)
                for half, s_fin in enumerate((s_fin_act, s_fin_dve)):
                    if b >= 2:
                        pe.wait_ge(s_fin, b - 1)
                    for j in range(2):
                        at = (2 * half + j) * P
                        mm = nc.tensor.transpose(ps[:, 2 * (b % 2) + half, j * P:(j + 1) * P], xT[:, b, at:at + P], ident_sb)
                    mm.then_inc(s_fin_mm, 1)

            run(pe, {"marks": marks, "turn_x": turn_x, "turn_ctx": turn_ctx, "k": k, "m": m, "v": v, "w": w,
                     "vw": vw_turn, "sums": sums, "scores": scores, "turn": turn, "output": output, "final": final})

        @block.scalar
        def _(act):
            act.dma_start(ranks_sb, ranks).then_inc(s_idx, 16)
            act.dma_start(ctx_sb[:], ctx.rearrange("b k d -> k b d")).then_inc(s_ctx, 16)

            def turn_x(_, b):
                act.wait_ge(s_xT_mm, b + 1)
                nc.scalar.copy(xT[:, b], ps[:, X_BANK]).then_inc(s_xT_act, 1)
                act.wait_ge(s_xT_act, b + 1)
                nc.scalar.copy(xT_hi[:, b], xT[:, b]).then_inc(s_xhi, 1)

            def keep_sums(l, b):
                act.wait_ge(s_norm_mm, b + 1)
                nc.scalar.copy(sumsq[:, TPB * b:TPB * (b + 1)], ps[:, SUMS_BANK, 0:TPB]).then_inc(s_sums, 1)

            def biased_output(l, b):
                if is_last(l) and b == BATCH - 1:
                    return
                act.wait_ge(s_bo, l + 1)
                if first(l) and b >= 1:
                    act.wait_ge(s_norm_mm, b)
                elif not first(l):
                    act.wait_ge(s_resid, l * BATCH + b)
                act.wait_ge(s_out, l * BATCH + (b + 1))
                nc.scalar.activation(xsq[:], ps[:, OUT_BANK], ACT.Identity, bias=bo_now[:]).then_inc(s_biased_out, 1)

            def split(l, b):
                act.wait_ge(s_resid, l * BATCH + (b + 1))
                nc.scalar.copy(xT_hi[:, b], xT[:, b]).then_inc(s_xhi, 1)

            def split_w(l, i):
                act.wait_ge(s_wk if i < 2 else s_wv, (l + 1) * 16)
                nc.scalar.copy(columns((wk_hi, wv_hi), i), columns((wk_sb, wv_sb), i)).then_inc(s_whi, 1)

            def split_q(l, _):
                act.wait_ge(s_wq, (l + 1) * 16)
                nc.scalar.copy(wq_hi[:], wq_sb[:]).then_inc(s_qhi, 1)

            def turn_ctx(l, _):
                for kc in range(KC):
                    act.wait_ge(s_ctx_mm, l * KC + (kc + 1))
                    nc.scalar.copy(ctx_hi[:, kc], ps[:, 2 + kc, 0:BK]).then_inc(s_ctx_hi, 1)

            def k(l, c):
                if skips_k(l, c):
                    return
                act.wait_ge(s_k_mm, has_k(l, c))
                nc.scalar.copy(kT_hi[:, c], ps[:, c % 2, 0:BK]).then_inc(s_khi, pairs_each(l))

            def v(l, c):
                act.wait_ge(s_v_mm, l * PAIRS + (c + 1))
                nc.scalar.copy(vT[:, c], ps[:, V_BANK, 0:BK]).then_inc(s_v, 1)

            def m(l, c):
                if c == 0:
                    act.wait_ge(s_scale, l + 1)
                for h in (2 * c, 2 * c + 1):
                    act.wait_ge(s_m_mm, l * HEADS + (h + 1))
                    nc.scalar.activation(m_hi[:, :, h], by_batch(ps[:, M_BANK + h % M_BANKS]), ACT.Copy, scale=scale_now[:]
                                         ).then_inc(s_mhi, 1)

            def w(l, c):
                for h in (2 * c, 2 * c + 1):
                    act.wait_ge(s_w_mm, l * HEADS + (h + 1))
                    nc.scalar.copy(vwT[:, :, h], by_batch(ps[:, TURN_BANK + h % 2])).then_inc(s_w, 1)

            def keep_vw(l, b):
                for q in range(NQ):
                    act.wait_ge(s_vw_mm, l * (NQ * BATCH) + (NQ * b + q + 1))
                    copy_quad(nc.scalar.copy, vw[:, b], q, ps[:, TURN_BANK + q]).then_inc(s_vw, 1)

            def exp(l, t):
                if t == 0:
                    act.wait_ge(s_inv, l + 1)
                act.wait_ge(s_shift, l * (2 * TILES) + 2 * (t + 1))
                nc.scalar.activation(prob[:, t % RING], prob[:, t % RING], ACT.Exp, scale=inv[:, t:t + 1]
                                     ).then_inc(s_exp, 1)

            def keep_pT(l, t):
                b, j = t // TPB, t % TPB
                if j == 0 and b >= 2:
                    act.wait_ge(s_out, l * BATCH + (b - 1))
                if t == 0 and not first(l):
                    act.wait_ge(s_out, l * BATCH)
                for q in range(NQ):
                    n = NQ * t + q
                    act.wait_ge(s_pT_mm, l * (NQ * TILES) + (n + 1))
                    copy_quad(nc.scalar.copy, pT[:, b % 2, :, j * P:(j + 1) * P], q, ps[:, TURN_BANK + q]
                              ).then_inc(s_pT, 1)

            def final(l, b):
                act.wait_ge(s_fin_mm, 2 * b + 1)
                nc.scalar.copy(out_rows(b, 0).rearrange("p t c -> p (t c)"), ps[:, 2 * (b % 2), 0:2 * C]
                               ).then_inc(s_fin_act, 1)

            run(act, {"split_w": split_w, "split_q": split_q, "turn_x": turn_x, "turn_ctx": turn_ctx, "k": k, "m": m,
                      "v": v, "w": w, "vw": keep_vw, "sums": keep_sums, "exp": exp, "turn": keep_pT,
                      "residual": biased_output, "split": split, "final": final})

        @block.vector
        def _(dve):
            done = [0]

            def chain(ins):
                done[0] += 1
                ins.then_inc(s_setup, 1)
                dve.wait_ge(s_setup, done[0])

            nc.vector.memset(xT[:, 0], 0.0).then_inc(s_zero, 1)
            dve.wait_ge(s_idx, 32)
            chain(nc.vector.tensor_copy(idx_f, idx_sb[:]))
            for w in range(2):
                last = nc.vector.tensor_scalar(hit[:, w], idx_f, key_sb[:, w:w + 1], None, ALU.is_equal)
            chain(last)
            chain(nc.vector.tensor_tensor(hit[:, 0], hit[:, 0], hit[:, 1], ALU.max))
            nc.vector.tensor_tensor(in_b, hit[:, 0, :, 2], hit[:, 0, :, 3], ALU.max)
            chain(nc.vector.tensor_tensor(in_a, hit[:, 0, :, 0], hit[:, 0, :, 1], ALU.max))
            chain(nc.vector.tensor_scalar(not_b, in_b, -1.0, 1.0, ALU.mult, ALU.add))
            chain(nc.vector.tensor_tensor(in_a, in_a, not_b, ALU.mult))
            nc.vector.tensor_tensor(marked, in_a, in_b, ALU.add).then_inc(s_marked, 1)
            dve.wait_ge(s_marked, 1)
            chain(nc.vector.tensor_scalar(plain, marked, -1.0, 1.0, ALU.mult, ALU.add))
            dve.wait_ge(s_cum_mm, 1)
            nc.vector.tensor_tensor(slot[:, 0], ps[0:KEYS, 4, 0:LAYERS], marked, ALU.mult)
            chain(nc.vector.scalar_tensor_tensor(slot[:, 1], ps[0:KEYS, 4, LAYERS:2 * LAYERS], key_sb[:, 0:1], plain,
                                                 ALU.add, ALU.mult))
            chain(nc.vector.tensor_tensor(slot[:, 2], slot[:, 0], slot[:, 1], ALU.add))
            for l in range(LAYERS):
                last = nc.vector.tensor_scalar(order[:, l], keys_sb, slot[:, 2, l:l + 1], None, ALU.is_equal)
            last.then_inc(s_order, 1)
            dve.wait_ge(s_order, 1)
            for side, of_side in enumerate((in_a, in_b)):
                last = nc.vector.tensor_tensor(sides[:, :, side], order[:, :, 0:MARKED],
                                               of_side.unsqueeze(2).to_broadcast([KEYS, LAYERS, MARKED]), ALU.mult)
            last.then_inc(s_sides, 1)
            dve.wait_ge(s_const, 16)
            chain(nc.vector.tensor_scalar(side_bias[:], mask_sb, 1.0, SUPPRESS, ALU.subtract, ALU.mult))

            def marks(_, n):
                dve.wait_ge(s_ind_mm, 1)
                nc.vector.tensor_copy(in_place[:].rearrange("p l s j -> p (l s j)"), ps[:, X_BANK, 0:LAYERS * 2 * MARKED]
                                      ).then_inc(s_ind, 1)
                dve.wait_ge(s_ind, 1)

            def token_bias(l, _):
                wide = [P, TPB, MARKED]
                for side, to in ((0, bias_a), (1, bias)):
                    last = nc.vector.tensor_tensor(to[:], side_bias[:, side].unsqueeze(2).to_broadcast(wide),
                                                   in_place[:, bass.ds(l, 1), side].to_broadcast(wide), ALU.mult)
                last.then_inc(s_bias, 1)
                dve.wait_ge(s_bias, l * 2 + 1)
                nc.vector.tensor_tensor(bias[:], bias[:], bias_a[:], ALU.add).then_inc(s_bias, 1)

            def scale(l, _):
                nc.vector.tensor_tensor(scale_now[:], small_sb[:, bass.ds(l, 1), NORM_W], small_sb[:, bass.ds(l, 1), SCALE],
                                        ALU.mult).then_inc(s_scale, 1)

            def split_w(l, i):
                if first(l):
                    dve.wait_ge(s_whi, i + 1)
                    nc.vector.tensor_tensor(columns((wk_lo, wv_lo), i), columns((wk_sb, wv_sb), i),
                                            columns((wk_hi, wv_hi), i).bitcast(F32), ALU.subtract).then_inc(s_wlo, 1)

            def turn_ctx(l, _):
                for kc in range(KC):
                    dve.wait_ge(s_ctx_hi, l * KC + (kc + 1))
                    nc.vector.tensor_tensor(ctx_lo[:, kc], ps[:, 2 + kc, 0:BK], ctx_hi[:, kc].bitcast(F32), ALU.subtract
                                            ).then_inc(s_ctx_lo, 1)

            def split_q(l, _):
                dve.wait_ge(s_qhi, l + 1)
                nc.vector.tensor_tensor(wq_lo[:], wq_sb[:], wq_hi[:].bitcast(F32), ALU.subtract).then_inc(s_qlo, 1)

            def k(l, c):
                if skips_k(l, c):
                    return
                dve.wait_ge(s_khi, has_k(l, c))
                nc.vector.tensor_tensor(kT_lo[:, c], ps[:, c % 2, 0:BK], kT_hi[:, c].bitcast(F32), ALU.subtract
                                        ).then_inc(s_klo, pairs_each(l))

            def m(l, c):
                for h in (2 * c, 2 * c + 1):
                    dve.wait_ge(s_mhi, l * HEADS + (h + 1))
                    nc.vector.scalar_tensor_tensor(m_lo[:, :, h], by_batch(ps[:, M_BANK + h % M_BANKS]), scale_now[:],
                                                   m_hi[:, :, h].bitcast(F32), ALU.mult, ALU.subtract).then_inc(s_mlo, 1)

            def norm(l, _):
                if normed(l):
                    dve.wait_ge(s_sums, BATCH)
                    nc.vector.tensor_scalar(msum[:], sumsq[:], 1.0 / C, NORM_EPS, ALU.mult, ALU.add).then_inc(s_msum, 1)
                nc.vector.tensor_copy(bo_now[:], small_sb[:, bass.ds(l, 1), BO]).then_inc(s_bo, 1)

            def add_bias(l, t):
                if t == 0:
                    dve.wait_ge(s_bias, l * 2 + 2)
                for half in range(2):
                    dve.wait_ge(s_scores, l * (2 * TILES) + (2 * t + half + 1))
                    places = half_banks(half)[:, :, :, 0:MARKED]
                    nc.vector.tensor_tensor(places, places, bias[:, t % TPB].unsqueeze(1).unsqueeze(1).to_broadcast(
                        [P, 2, HPB, MARKED]), ALU.add).then_inc(s_biased, 1)

            def shift(l, t):
                at = l * (2 * TILES) + 2 * t
                own_max = [mx[:, t % RING, HALF * half:HALF * (half + 1)].rearrange("p (a h) -> p a h", a=2)
                           for half in range(2)]
                for half in range(2):
                    dve.wait_ge(s_biased, at + (half + 1))
                    nc.vector.tensor_reduce(own_max[half], half_banks(half), AX.X, ALU.max).then_inc(s_max, 1)
                if t >= RING:
                    dve.wait_ge(s_pT_mm, l * (NQ * TILES) + NQ * (t - RING + 1))
                for half in range(2):
                    dve.wait_ge(s_max, at + (half + 1))
                    to = prob[:, t % RING, HALF * KEYS * half:HALF * KEYS * (half + 1)]
                    nc.vector.tensor_tensor(to.rearrange("p (a h k) -> p a h k", a=2, k=KEYS), half_banks(half),
                                            own_max[half].unsqueeze(3).to_broadcast([P, 2, HPB, KEYS]),
                                            ALU.subtract).then_inc(s_shift, 1)

            def denominators(l, t):
                dve.wait_ge(s_exp, l * TILES + (t + 1))
                nc.vector.tensor_reduce(tot[:, t % RING], by_head(prob[:, t % RING]), AX.X, ALU.add).then_inc(s_sum, 1)

            def reciprocals(l, t):
                dve.wait_ge(s_sum, l * TILES + (t + 1))
                nc.vector.reciprocal(rec[:, t % RING], tot[:, t % RING]).then_inc(s_rec, 1)

            def last_residual(l, b):
                if is_last(l) and b == BATCH - 1:
                    dve.wait_ge(s_out, l * BATCH + (b + 1))
                    dve.wait_ge(s_resid, l * BATCH + b)
                    nc.vector.scalar_tensor_tensor(xT[:, b], ps[:, OUT_BANK], bo_now[:], xT[:, b], ALU.add, ALU.add
                                                   ).then_inc(s_resid, 1)

            def final(l, b):
                dve.wait_ge(s_fin_mm, 2 * b + 2)
                nc.vector.tensor_copy(out_rows(b, 1).rearrange("p t c -> p (t c)"), ps[:, 2 * (b % 2) + 1, 0:2 * C]
                                      ).then_inc(s_fin_dve, 1)

            run(dve, {"marks": marks, "bias": token_bias, "scale": scale, "split_w": split_w, "split_q": split_q,
                      "turn_ctx": turn_ctx, "k": k, "m": m, "norm": norm, "scores": add_bias, "shift": shift,
                      "exp": denominators, "normalise": reciprocals, "residual": last_residual, "final": final})

        @block.gpsimd
        def _(pool):
            nc.gpsimd.memset(ones[:], 1.0)
            nc.gpsimd.memset(key_ones, 1.0)
            nc.gpsimd.memset(halfs[:], -0.5).then_inc(s_half, 1)
            pool.wait_ge(s_half, 1)

            def turn_x(_, b):
                pool.wait_ge(s_xhi, b + 1)
                nc.gpsimd.tensor_tensor(xT_lo[:, b], xT[:, b], xT_hi[:, b].bitcast(F32), ALU.subtract).then_inc(s_xlo, 1)

            def split_w(l, i):
                if first(l):
                    return
                pool.wait_ge(s_whi, l * 4 + (i + 1))
                nc.gpsimd.tensor_tensor(columns((wk_lo, wv_lo), i), columns((wk_sb, wv_sb), i),
                                        columns((wk_hi, wv_hi), i).bitcast(F32), ALU.subtract).then_inc(s_wlo, 1)

            def residual(l, b):
                if is_last(l) and b == BATCH - 1:
                    return
                pool.wait_ge(s_biased_out, l * BATCH + (b + 1))
                nc.gpsimd.tensor_tensor(xT[:, b], xT[:, b], xsq[:], ALU.add).then_inc(s_resid, 1)

            def split(l, b):
                pool.wait_ge(s_resid, l * BATCH + (b + 1))
                if first(l):
                    nc.gpsimd.tensor_tensor(xsq[:], xT[:, b], xT[:, b], ALU.mult).then_inc(s_xsq, 1)
                pool.wait_ge(s_xhi, (l + 1) * BATCH + (b + 1))
                nc.gpsimd.tensor_tensor(xT_lo[:, b], xT[:, b], xT_hi[:, b].bitcast(F32), ALU.subtract).then_inc(s_xlo, 1)

            def norm(l, _):
                if normed(l):
                    pool.wait_ge(s_msum, 1)
                    nc.gpsimd.tensor_tensor(inv[:], msum[:], halfs[:], ALU.pow).then_inc(s_inv, 1)
                else:
                    nc.gpsimd.memset(inv[:], 1.0).then_inc(s_inv, 1)

            def normalise(l, t):
                pool.wait_ge(s_rec, l * TILES + (t + 1))
                nc.gpsimd.tensor_tensor(by_head(prob[:, t % RING]), by_head(prob[:, t % RING]),
                                        rec[:, t % RING].unsqueeze(2).to_broadcast([P, HEADS, KEYS]),
                                        ALU.mult).then_inc(s_prob, 1)

            run(pool, {"split_w": split_w, "turn_x": turn_x, "norm": norm, "normalise": normalise,
                       "residual": residual, "split": split})


def copy_quad(copy, dst, q, bank):
    full = [c for c in range(4 * q, min(4 * q + 4, len(CHUNKS))) if CHUNKS[c][1] == P]
    last = copy(dst[:, full[0]:full[-1] + 1], bank[:, 0:len(full) * P].rearrange("p (c n) -> p c n", n=P))
    for c in range(4 * q + len(full), min(4 * q + 4, len(CHUNKS))):
        rows, at = CHUNKS[c][1], (c - 4 * q) * P
        last = copy(dst[0:rows, c], bank[0:rows, at:at + P])
    return last


def lay_out(inputs):
    import numpy as np

    def heads64(w, axis):
        shape = list(w.shape)
        shape[axis:axis + 1] = [HEADS, HDIM]
        full = np.zeros(shape, w.dtype)
        small = list(w.shape)
        small[axis:axis + 1] = [HEADS, w.shape[axis] // HEADS]
        at = [slice(None)] * len(shape)
        at[axis + 1] = slice(0, w.shape[axis] // HEADS)
        full[tuple(at)] = w.reshape(small)
        shape = list(w.shape)
        shape[axis] = INNER
        return full.reshape(shape)

    def repeated(w, times):
        d = w.shape[1] // 4
        full = np.zeros((w.shape[0], HEADS, d), w.dtype)
        full[:, 0:4 * times] = np.repeat(w.reshape(w.shape[0], 4, d), times, axis=1)
        return full.reshape(w.shape[0], HEADS * d)

    big = ("L0_xattn_", "L2_xattn_", "L3_xattn_")
    a = {k: np.asarray(v) for k, v in inputs.items()}

    def stack(name, one):
        return np.stack([a[big[0] + name], one, a[big[1] + name], a[big[2] + name]])

    d = {"x": a["x"], "ctx": a["ctx_2048"]}
    d["wq"] = stack("Wq", heads64(a["L1_xattn_wq"], 1)).transpose(0, 2, 1)
    d["wk"] = stack("Wk", heads64(repeated(a["L1_xattn_wk"], 2), 1))
    d["wv"] = stack("Wv", heads64(repeated(a["L1_xattn_wv"], 4), 1))
    d["wo"] = stack("Wo", heads64(a["L1_xattn_wo"], 0))
    zeros, ones = np.zeros((C,), np.float32), np.ones((C,), np.float32)
    small = np.zeros((P, LAYERS, 3), np.float32)
    small[:, :, NORM_W] = np.stack([ones, a["L1_xattn_norm_w"], ones, ones], axis=1)
    small[:, :, SCALE] = HDIM ** -0.5
    small[:, NORMED, SCALE] = (C // HEADS) ** -0.5
    small[:, :, BO] = stack("bo", zeros).T
    none = np.full((2,), -1000, np.int32)
    rows = [np.concatenate([a[name + "token_indices_A"], a[name + "token_indices_B"]] if name else [none, none])
            for name in ("L0_xattn_", None, "L2_xattn_", "L3_xattn_")]
    d["idx"] = np.broadcast_to(np.stack(rows), (KEYS, LAYERS, 4))
    masks = np.stack([a["mask_S_fk1"], a["mask_S_fk0"]]).reshape(2, TPB, P).transpose(2, 0, 1)
    d["vectors"] = np.concatenate([np.eye(P, dtype=np.float32), small.reshape(P, -1), masks.reshape(P, -1)], axis=1)
    at = np.arange(KEYS, dtype=np.float32)
    d["ranks"] = np.concatenate([np.stack([at, at - KEYS], axis=1), np.broadcast_to(at, (KEYS, KEYS)),
                                 (at[:, None] < at[None, :]), (at[:, None] >= at[None, :])], axis=1).astype(np.float32)
    return d


def kernel(**inputs):
    import numpy as np
    import concourse.bacc as bacc
    from concourse.bass_utils import run_bass_kernel_spmd

    nc = bacc.Bacc("TRN2", target_bir_lowering=False, num_devices=1)
    arrays, aps = {}, {}
    for name, value in lay_out(inputs).items():
        value = np.ascontiguousarray(value)
        arrays[f"in_{name}"] = value
        aps[name] = nc.dram_tensor(f"in_{name}", value.shape, mybir.dt.from_np(value.dtype), kind="ExternalInput").ap()
    out = nc.dram_tensor("out_x", (BATCH, SEQ, C), F32, kind="ExternalOutput").ap()
    build(nc, out=out, **aps)
    result = run_bass_kernel_spmd(nc, [arrays], core_ids=[0])
    return result.results[0]["out_x"]
```
